# Optimizing a Trainium2 kernel written in Bass

```python
import numpy as np
import jax
import jax.numpy as jnp

def _softmax(x, axis=-1):
    return jax.nn.softmax(x, axis=axis)

def _gelu(x):
    return jax.nn.gelu(x, approximate=True)

def _silu(x):
    return jax.nn.silu(x)

def _sigmoid(x):
    return jax.nn.sigmoid(x)

def _layernorm(x, axis=-1, eps=1e-05):
    m = jnp.mean(x, axis=axis, keepdims=True)
    v = jnp.var(x, axis=axis, keepdims=True)
    return (x - m) / jnp.sqrt(v + eps)

def _scatter_add(tgt, idx, src, axis=0):
    return tgt.at[idx].add(src)

def _segment_sum(src, seg, n):
    return jax.ops.segment_sum(src, seg, n)
kernel_name = 'mk_adj_resnorm_d2_adj_r2_983db1'

def setup_inputs(seed: int=0):
    np.random.seed(seed)
    _w = jnp.asarray

    def _rec_inputs():
        import jax
        import jax.numpy as jnp
        _gk = jax.random.key(seed)
        x = -9.806e-05 + 1 * jax.random.normal(jax.random.fold_in(_gk, 1), (4096, 64), jnp.float32)
        _a = jax.random.bernoulli(jax.random.fold_in(_gk, 2), 0.000488281, (4096, 4096))
        _af = _a.astype(jnp.float32)
        adj = _af
        return (x, adj)
    x, adj = _rec_inputs()

    def _L0_gnn_setup():
        import jax, jax.numpy as jnp
        import numpy as np
        N = 4096
        D = 64
        key = jax.random.key(seed)
        ks = jax.random.split(key, 13)
        s = 0.05
        return {'object_features': jax.random.normal(ks[0], (N, D), dtype=jnp.float32), 'relationship_features': jax.random.normal(ks[1], (N, D), dtype=jnp.float32), 'adjacency_matrix': (jax.random.uniform(ks[2], (N, N)) < 0.05).astype(jnp.float32), 'W_obj': jax.random.normal(ks[3], (D, D), dtype=jnp.float32) * s, 'b_obj': jax.random.normal(ks[4], (D,), dtype=jnp.float32) * s, 'W_nobj': jax.random.normal(ks[5], (D, D), dtype=jnp.float32) * s, 'b_nobj': jax.random.normal(ks[6], (D,), dtype=jnp.float32) * s, 'W_rel': jax.random.normal(ks[7], (D, D), dtype=jnp.float32) * s, 'b_rel': jax.random.normal(ks[8], (D,), dtype=jnp.float32) * s, 'W_skip': jax.random.normal(ks[9], (D, D), dtype=jnp.float32) * s, 'b_skip': jax.random.normal(ks[10], (D,), dtype=jnp.float32) * s, 'Wa_w': jax.random.normal(ks[11], (2 * D, 1), dtype=jnp.float32) * s, 'Wa_b': jax.random.normal(ks[12], (1,), dtype=jnp.float32) * s}
    _L0_gnn_all = _L0_gnn_setup()
    _L0_gnn_in = {k: v for k, v in _L0_gnn_all.items() if k in ('relationship_features', 'W_obj', 'b_obj', 'W_nobj', 'b_nobj', 'W_rel', 'b_rel', 'W_skip', 'b_skip', 'Wa_w', 'Wa_b')}
    del _L0_gnn_all

    def _L1_gnn_setup():
        import jax, jax.numpy as jnp
        import numpy as np
        N, D_IN, D_OUT = (4096, 64, 64)
        MAX_NEIGH = 100
        DECAY = 0.5
        key = jax.random.key(seed)
        k1, k2, k3, k4 = jax.random.split(key, 4)
        stdv = 1.0 / np.sqrt(D_OUT)
        inputs = {'input': jax.random.normal(k1, (N, D_IN), dtype=jnp.float32), 'adj': jax.random.randint(k2, (N, N), 0, 2).astype(jnp.float32), 'weight': jax.random.uniform(k3, (D_IN, D_OUT), minval=-stdv, maxval=stdv, dtype=jnp.float32), 'bias': jax.random.uniform(k4, (D_OUT,), minval=-stdv, maxval=stdv, dtype=jnp.float32)}
        return inputs
    _L1_gnn_all = _L1_gnn_setup()
    _L1_gnn_in = {k: v for k, v in _L1_gnn_all.items() if k in ('weight', 'bias')}
    del _L1_gnn_all
    return {'x': x, 'adj': adj, 'L0_gnn_relationship_features': _L0_gnn_in['relationship_features'], 'L0_gnn_W_obj': _L0_gnn_in['W_obj'], 'L0_gnn_b_obj': _L0_gnn_in['b_obj'], 'L0_gnn_W_nobj': _L0_gnn_in['W_nobj'], 'L0_gnn_b_nobj': _L0_gnn_in['b_nobj'], 'L0_gnn_W_rel': _L0_gnn_in['W_rel'], 'L0_gnn_b_rel': _L0_gnn_in['b_rel'], 'L0_gnn_W_skip': _L0_gnn_in['W_skip'], 'L0_gnn_b_skip': _L0_gnn_in['b_skip'], 'L0_gnn_Wa_w': _L0_gnn_in['Wa_w'], 'L0_gnn_Wa_b': _L0_gnn_in['Wa_b'], 'L1_gnn_weight': _L1_gnn_in['weight'], 'L1_gnn_bias': _L1_gnn_in['bias']}

def reference(x, adj, L0_gnn_relationship_features, L0_gnn_W_obj, L0_gnn_b_obj, L0_gnn_W_nobj, L0_gnn_b_nobj, L0_gnn_W_rel, L0_gnn_b_rel, L0_gnn_W_skip, L0_gnn_b_skip, L0_gnn_Wa_w, L0_gnn_Wa_b, L1_gnn_weight, L1_gnn_bias):
    import jax
    import jax.numpy as jnp

    def _L0_gnn_ref(object_features, relationship_features, adjacency_matrix, W_obj, b_obj, W_nobj, b_nobj, W_rel, b_rel, W_skip, b_skip, Wa_w, Wa_b):
        import jax, jax.numpy as jnp
        import numpy as np
        N = 4096
        D = 64
        x, r, A = (object_features, relationship_features, adjacency_matrix)
        d = x.shape[1]
        msgs_obj = x @ W_obj + b_obj
        msgs_nbr = A.T @ (x @ W_nobj + b_nobj)
        msgs_rel = r @ W_rel + b_rel
        aggregated = msgs_obj + msgs_nbr + msgs_rel
        sx = x @ Wa_w[:d]
        sr = r @ Wa_w[d:]
        scores = (sx + sr.T + Wa_b) * A
        attention = jax.nn.softmax(scores, axis=1)
        attn_agg = jnp.einsum('ij,ik->ik', attention, aggregated)
        return x @ W_skip + b_skip + attn_agg

    def _L1_gnn_ref(input, adj, weight, bias):
        import jax, jax.numpy as jnp
        import numpy as np
        N, D_IN, D_OUT = (4096, 64, 64)
        MAX_NEIGH = 100
        DECAY = 0.5
        support = input @ weight
        mask = (adj != 0).astype(support.dtype)
        rank = jnp.cumsum(mask, axis=1)
        deg = rank[:, -1:]
        k = jnp.minimum(deg, float(MAX_NEIGH))
        pos = rank - (deg - k)
        w = mask * jnp.where(pos > 0, DECAY ** (k - pos), 0.0)
        out = w @ support + bias
        return out
    x = _layernorm(x + _L0_gnn_ref(x, L0_gnn_relationship_features, adj, L0_gnn_W_obj, L0_gnn_b_obj, L0_gnn_W_nobj, L0_gnn_b_nobj, L0_gnn_W_rel, L0_gnn_b_rel, L0_gnn_W_skip, L0_gnn_b_skip, L0_gnn_Wa_w, L0_gnn_Wa_b), axis=-1)
    x = _layernorm(x + _L1_gnn_ref(x, adj, L1_gnn_weight, L1_gnn_bias), axis=-1)
    return x

_drawn_inputs = setup_inputs


def setup_inputs(seed=0):
    import zlib

    import numpy as np

    out = dict(_drawn_inputs(seed))
    spreads = {}
    factors = {}
    for name, (base, spread) in spreads.items():
        noise = np.random.default_rng([zlib.crc32(name.encode()), seed]).standard_normal(out[name].shape)
        drawn = base * np.exp(spread * noise) if base else spread * noise
        out[name] = jnp.asarray(drawn.astype(out[name].dtype))
    for name, factor in factors.items():
        out[name] = (out[name] * factor).astype(out[name].dtype)
    return out
```

```python
from contextlib import ExitStack

import concourse.bass as bass
from concourse import mybir
from concourse.alu_op_type import AluOpType as ALU

N, D, P = 4096, 64, 128
TILES = N // P
GT = 4
GROUPS = TILES // GT
QB = 8
UNITS = TILES // QB
QC = QB * P
ZC = 512
GW = GT * P
PAIRS = GROUPS // 2
PT = 2 * GT
MAX_NEIGH = 100
EPS = 1e-5
STEP = 128.0
OWN = 16384.0
SHIFT = 2.0 ** (127 - MAX_NEIGH)
ON = 2.0
WCOLS = 2 * D + 2


def build(nc, x, adj, rel, W_obj, b_obj, W_nobj, b_nobj, W_rel, b_rel, W_skip, b_skip, Wa_w, Wa_b,
          W_l1, b_l1, out):
    fp32, bf16, u16 = mybir.dt.float32, mybir.dt.bfloat16, mybir.dt.uint16
    ACT = mybir.ActivationFunctionType
    AX = mybir.AxisListType.X
    es = ExitStack()
    with es:
        def sb(name, shape, dt):
            return es.enter_context(nc.sbuf_tensor(name, shape, dt))

        def sem(name):
            return es.enter_context(nc.semaphore(name))

        packed = sb("packed", [P, GROUPS, TILES, P], u16)
        area_a = sb("area_a", [P, UNITS, GT, QC], fp32)
        stage = area_a[:, :, :, :].rearrange("p u t c -> p (u t c)").bitcast(u16).rearrange(
            "p (a b t c) -> p a b t c", a=2, b=TILES, t=GT)
        stage_bf = area_a[:, :, :, :].rearrange("p u t c -> p (u t c)").bitcast(bf16).rearrange(
            "p (a b i) -> p a b i", a=2, b=TILES)
        area_p = sb("area_p", [P, GT * QC], fp32)
        scores = area_p[:, :].rearrange("p (t c) -> p t c", t=GT)
        xr = area_p[:, :].rearrange("p (t c) -> p t c", t=TILES)
        x1 = area_p[:, 0:TILES * D].rearrange("p (t d) -> p t d", t=TILES)
        x1b = area_p[:, TILES * D:2 * TILES * D].rearrange("p (t d) -> p t d", t=TILES)
        area_y = sb("area_y", [P, TILES, D], fp32)
        base = sb("base", [P, TILES, D], fp32)
        parts = sb("parts", [P, TILES, 3 * D], bf16)
        area_z = sb("area_z", [P, 2, N], bf16)
        z_cols, z_rows = area_z[:, 0, :], area_z[:, 1, :]
        weights = area_z[:, 0, 0:2 * 2 * GW].bitcast(u16).rearrange("p (a s i) -> p a s i", a=2, s=2)
        weights_bf = area_z[:, 0, 0:2 * 2 * GW].rearrange("p (a s i) -> p a s i", a=2, s=2)
        x1t = area_z[0:D, 1, 0:2 * QC].bitcast(fp32)
        xrt = sb("xrt", [P, 2, GW], fp32)
        tmp_a = xrt[:, 0, :].rearrange("p (t d) -> p t d", t=QB)
        tmp_b = xrt[:, 1, :].rearrange("p (t d) -> p t d", t=QB)
        supp = sb("supp", [P, QB, D], fp32)
        rest = sb("rest", [P, QB, D], fp32)
        rest_y = sb("rest_y", [P, GT, D], fp32)
        identf = sb("identf", [P, P], fp32)
        ident = sb("ident", [P, GT, P], bf16)
        upto = sb("upto", [P, P], bf16)
        beyond = sb("beyond", [P, P], bf16)
        w_all = sb("w_all", [P, WCOLS], fp32)
        w_agg = sb("w_agg", [P, D], fp32)
        w_l1 = sb("w_l1", [D, D], fp32)
        bias = sb("bias", [P, 6, D], fp32)
        wab = sb("wab", [P, 1], fp32)
        floor = sb("floor", [P, 1], fp32)
        cs = sb("cs", [P, 2, TILES], fp32)
        cs_rest = sb("cs_rest", [P, 2, TILES], fp32)
        cs_parts = sb("cs_parts", [P, 2, TILES, 6], bf16)
        top = sb("top", [P, GT, 2], fp32)
        negmax = sb("negmax", [P, TILES, UNITS], fp32)
        sums = sb("sums", [P, TILES, UNITS], fp32)
        small = sb("small", [P, 8, TILES], fp32)
        share = sb("share", [P, TILES, UNITS], fp32)
        ln = sb("ln", [P, 8, QB], fp32)

        acc = [es.enter_context(nc.psum_tensor(f"acc{i}", [P, 512], fp32)) for i in range(4)]
        zb = [es.enter_context(nc.psum_tensor(f"zb{i}", [P, 512], fp32)) for i in range(2)]
        tb = [es.enter_context(nc.psum_tensor(f"tb{i}", [P, 512], fp32)) for i in range(2)]

        xr_loaded, w_loaded, zeroed = sem("xr_loaded"), sem("w_loaded"), sem("zeroed")
        consts = sem("consts")
        a_loaded = [sem(f"a_loaded{q}") for q in range(UNITS)]
        xrt_ready, xrt_saved, proj_ready, proj_saved = sem("xrt_ready"), sem("xrt_saved"), sem("proj_ready"), sem("proj_saved")
        skip_ready, cs_ready, zt_ready, zt_saved = sem("skip_ready"), sem("cs_ready"), sem("zt_ready"), sem("zt_saved")
        y_saved, y_split = sem("y_saved"), sem("y_split")
        z_ready, z_free = sem("z_ready"), sem("z_free")
        t_ready, t_free = sem("t_ready"), sem("t_free")
        unit_read = sem("unit_read")
        max_ready, p_free = sem("max_ready"), sem("p_free")
        share_in, share_out = sem("share_in"), sem("share_out")
        var_ready, std_ready = sem("var_ready"), sem("std_ready")
        x1_ready, x1t_ready, x1t_saved = sem("x1_ready"), sem("x1t_ready"), sem("x1t_saved")
        s_ready, s_saved, s_split = sem("s_ready"), sem("s_saved"), sem("s_split")
        x1b_ready = sem("x1b_ready")
        staged = sem("staged")
        v_ready, w_ready, w_used = sem("v_ready"), sem("w_ready"), sem("w_used")
        acc_free = sem("acc_free")
        out_ready, out_done = sem("out_ready"), sem("out_done")
        dve_done, pool_done = sem("dve_done"), sem("pool_done")
        passed, passed_pool = sem("passed"), sem("passed_pool")

        adj_v = adj.rearrange("(g t p) c -> p g t c", t=GT, p=P)
        x_v = x.rearrange("(t p) d -> p t d", p=P)
        r_v = rel.rearrange("(t p) d -> p t d", p=P)
        out_v = out.rearrange("(t p) d -> p t d", p=P)

        def block_t(q, t, b):
            v = area_a[:, q, t, b * P:(b + 1) * P].bitcast(bf16)
            return v.rearrange("p (c h) -> p c h", h=2)[:, :, 1]

        block = es.enter_context(nc.Block())

        @block.sync
        def _(sp):
            sp.dma_start(xr[:, :, 0:D], x_v).then_inc(xr_loaded, 16)
            sp.dma_start(xr[:, :, D:2 * D], r_v).then_inc(xr_loaded, 16)
            for q in range(UNITS):
                sp.dma_start(area_a[:, q, :, :], adj_v[:, 0, :, q * QC:(q + 1) * QC]).then_inc(a_loaded[q], 16)
            with sp.Fori(1, GROUPS) as g:
                for q in range(UNITS):
                    sp.wait_ge(unit_read, g * UNITS + (q + 1 - UNITS))
                    sp.wait_ge(z_free, (g * UNITS + (q + 1 - UNITS)) * QB + 2)
                    sp.dma_start(area_a[:, q, :, :], adj_v[:, bass.ds(g, 1), :, q * QC:(q + 1) * QC].rearrange("p g t c -> p (g t) c")).then_inc(a_loaded[q], 16)
            with sp.Fori(0, PAIRS) as g:
                sp.wait_ge(out_ready, g + 2)
                sp.dma_start(out_v[:, bass.ds(g * PT, PT), :], x1b[:, bass.ds(g * PT, PT), :]).then_inc(out_done, 16)
            sp.wait_ge(out_done, 16 * PAIRS)

        @block.gpsimd
        def _(pool):
            count = [0]

            def link(ins):
                count[0] += 1
                ins.then_inc(pool_done, 1)
                pool.wait_ge(pool_done, count[0])

            nc.gpsimd.memset(w_all[:], 0.0).then_inc(zeroed, 1)
            nc.gpsimd.memset(identf[:], 0.0)
            for t in range(GT):
                nc.gpsimd.memset(ident[:, t, :], 0.0)
            nc.gpsimd.memset(floor[:], STEP * (MAX_NEIGH + 1) - OWN)
            nc.gpsimd.memset(upto[:], -STEP / ON)
            link(nc.gpsimd.memset(beyond[:], -STEP / ON))

            def diagonal(tile, fill):
                return nc.gpsimd.affine_select(out=tile, in_=tile, compare_op=ALU.not_equal, fill=fill, base=0,
                                               pattern=[[-1, P]], channel_multiplier=1)

            diagonal(identf[:, :], 1.0)
            for t in range(GT):
                diagonal(ident[:, t, :], 2.0 ** t)
            nc.gpsimd.affine_select(out=upto[:, :], in_=upto[:, :], compare_op=ALU.is_ge, fill=0.0, base=0,
                                    pattern=[[-1, P]], channel_multiplier=1)
            link(nc.gpsimd.affine_select(out=beyond[:, :], in_=beyond[:, :], compare_op=ALU.is_ge, fill=0.0, base=0,
                                         pattern=[[1, P]], channel_multiplier=-1))
            diagonal(upto[:, :], (OWN - STEP) / ON)
            diagonal(beyond[:, :], -OWN / ON).then_inc(consts, 1)
            nc.gpsimd.memset(area_z[:, :, :], 0.0).then_inc(zeroed, 1)
            pool.wait_ge(w_loaded, 16 * 13)
            pool.wait_ge(xr_loaded, 32)
            nc.gpsimd.tensor_tensor(bias[:, 5, :], bias[:, 2, :], bias[:, 3, :], ALU.add)
            nc.gpsimd.tensor_tensor(base[:, :, :], xr[:, :, 0:D], bias[:, 1:2, :].broadcast_to([P, TILES, D]), ALU.add).then_inc(skip_ready, 1)
            done = count[0]
            with pool.Fori(0, GROUPS) as g:
                y = area_y[:, bass.ds(g * GT, GT), :]
                hi, mid, lo = (parts[:, bass.ds(g * GT, GT), k * D:(k + 1) * D] for k in range(3))
                pool.wait_ge(y_saved, g + 1)
                pool.sem_inc(passed_pool, 1)
                nc.gpsimd.tensor_copy(hi, y).then_inc(pool_done, 1)
                pool.wait_ge(pool_done, g * 4 + (done + 1))
                pool.sem_inc(passed_pool, 1)
                nc.gpsimd.tensor_tensor(rest_y[:, :, :], y, hi, ALU.subtract).then_inc(pool_done, 1)
                pool.wait_ge(pool_done, g * 4 + (done + 2))
                pool.sem_inc(passed_pool, 1)
                nc.gpsimd.tensor_copy(mid, rest_y[:, :, :]).then_inc(pool_done, 1)
                pool.wait_ge(pool_done, g * 4 + (done + 3))
                pool.sem_inc(passed_pool, 1)
                nc.gpsimd.tensor_tensor(lo, rest_y[:, :, :], mid, ALU.subtract).then_inc(y_split, 1)
                pool.wait_ge(y_split, g + 1)
                pool.sem_inc(passed_pool, 1)
                nc.gpsimd.tensor_copy(rest_y[:, :, 0:1], rest_y[:, :, 0:1]).then_inc(pool_done, 1)
            for n, m in enumerate(reversed(range(4))):
                pool.wait_ge(x1_ready, n + 1)
                rows = slice(m * QB, (m + 1) * QB)
                nc.gpsimd.tensor_tensor(x1b[:, rows, :], x1[:, rows, :], bias[:, 4:5, :].broadcast_to([P, QB, D]), ALU.add).then_inc(x1b_ready, 1)

        @block.scalar
        def _(act):
            act.dma_start(bias[:, 0, :], b_nobj.partition_broadcast(P)).then_inc(w_loaded, 16)
            act.dma_start(bias[:, 1, :], b_skip.partition_broadcast(P)).then_inc(w_loaded, 16)
            act.dma_start(bias[:, 2, :], b_obj.partition_broadcast(P)).then_inc(w_loaded, 16)
            act.dma_start(bias[:, 3, :], b_rel.partition_broadcast(P)).then_inc(w_loaded, 16)
            act.dma_start(bias[:, 4, :], b_l1.partition_broadcast(P)).then_inc(w_loaded, 16)
            act.dma_start(wab[:, :], Wa_b.partition_broadcast(P)).then_inc(w_loaded, 16)
            act.dma_start(w_agg[0:D, :], W_obj).then_inc(w_loaded, 16)
            act.dma_start(w_agg[D:P, :], W_rel).then_inc(w_loaded, 16)
            act.dma_start(w_l1[:, :], W_l1).then_inc(w_loaded, 16)
            act.wait_ge(zeroed, 1)
            act.dma_start(w_all[0:D, 0:D], W_nobj).then_inc(w_loaded, 16)
            act.dma_start(w_all[0:D, D:2 * D], W_skip).then_inc(w_loaded, 16)
            act.dma_start(w_all[0:D, 2 * D:2 * D + 1], Wa_w[0:D, :]).then_inc(w_loaded, 16)
            act.dma_start(w_all[D:P, 2 * D + 1:2 * D + 2], Wa_w[D:2 * D, :]).then_inc(w_loaded, 16)
            for k in range(GROUPS):
                act.wait_ge(xrt_ready, k + 1)
                if k >= 2:
                    act.wait_ge(proj_ready, k - 1)
                nc.scalar.activation(xrt[:, k % 2, :], tb[k % 2][:, :], ACT.Copy).then_inc(xrt_saved, 1)
            act.wait_ge(zeroed, 2)
            for k in range(4):
                act.wait_ge(zt_ready, 2 * k + 1)
                nc.scalar.activation(z_cols[0:6, k * QC:(k + 1) * QC], tb[0][:, :].bitcast(bf16)[0:6, :], ACT.Copy).then_inc(zt_saved, 1)
            act.wait_ge(zt_saved, 8)
            act.sem_inc(t_free, 2)
            act.sem_inc(p_free, GT)
            with act.Fori(0, GROUPS) as g:
                for q in range(UNITS):
                    for t in range(GT):
                        act.wait_ge(max_ready, g * (UNITS * GT) + (q * GT + t + 1))
                        nc.scalar.activation(scores[:, t, :], scores[:, t, :], ACT.Exp,
                                             bias=negmax[:, bass.ds(g * GT + t, 1), q],
                                             accum_out=sums[:, bass.ds(g * GT + t, 1), q]).then_inc(p_free, 1)
                        if t % 2:
                            s = t // 2
                            act.wait_ge(t_ready, g * (2 * UNITS) + (2 * q + s + 1))
                            nc.scalar.activation(
                                packed[:, bass.ds(g, 1), q * QB + s * 4:q * QB + s * 4 + 4, :].rearrange("p g b i -> p (g b i)"),
                                tb[s][:, :], ACT.Copy).then_inc(t_free, 1)
            act.wait_ge(share_in, 1)
            nc.scalar.activation(share[:, :, :], share[:, :, :], ACT.Exp).then_inc(share_out, 1)

            def std(n):
                act.wait_ge(var_ready, n + 1)
                nc.scalar.activation(ln[:, 2, :], ln[:, 1, :], ACT.Sqrt).then_inc(std_ready, 1)

            def save_x1t(n):
                for s in range(2):
                    act.wait_ge(x1t_ready, 2 * n + s + 1)
                    if s == 0 and n:
                        act.wait_ge(s_ready, n)
                    nc.scalar.activation(x1t[:, s * 512:(s + 1) * 512], tb[s][0:D, :], ACT.Copy).then_inc(x1t_saved, 1)

            def save_support(n, m):
                act.wait_ge(s_ready, n + 1)
                if n:
                    act.wait_ge(s_split, n)
                nc.scalar.activation(supp[:, :, :].rearrange("p t d -> p (t d)"), tb[0][:, :], ACT.Copy, scale=SHIFT).then_inc(s_saved, 1)
                act.wait_ge(s_saved, 2 * n + 1)
                nc.scalar.activation(parts[:, m * QB:(m + 1) * QB, 0:D], supp[:, :, :], ACT.Copy).then_inc(s_saved, 1)

            def weigh(p, b, a, first):
                n = 2 * (TILES - 1 - b) + a
                act.wait_ge(v_ready, p * (2 * TILES) + (n + 1))
                if not (first and n < 4):
                    act.wait_ge(w_used, p * (2 * TILES) + (n - 3))
                nc.scalar.activation(weights[:, a, b % 2, :], zb[a][:, :], ACT.Relu, bias=floor[:, 0:1]).then_inc(w_ready, 1)

            std(0)
            save_x1t(0)
            save_support(0, 3)
            for b in reversed(range(TILES)):
                for a in range(2):
                    weigh(0, b, a, True)
                if b >= QB:
                    n = 4 - b // QB
                    if b % QB == 7:
                        std(n)
                    if b % QB == 5:
                        save_x1t(n)
                    if b % QB == 4:
                        save_support(n, 3 - n)
            with act.Fori(1, PAIRS) as p:
                for b in reversed(range(TILES)):
                    for a in range(2):
                        weigh(p, b, a, False)
                    if b == TILES - 4:
                        act.wait_ge(var_ready, p + 4)
                        nc.scalar.activation(ln[:, 2, :], ln[:, 1, :], ACT.Sqrt).then_inc(std_ready, 1)
            std(4 + PAIRS - 1)

        @block.vector
        def _(dve):
            count = [0]

            def link(ins):
                count[0] += 1
                ins.then_inc(dve_done, 1)
                dve.wait_ge(dve_done, count[0])

            dve.wait_ge(skip_ready, 1)
            for k in range(GROUPS):
                dve.wait_ge(proj_ready, k + 1)
                for h in range(2):
                    rows = slice(k * GT + 2 * h, k * GT + 2 * h + 2)
                    z = zb[h][:, 0:2 * WCOLS].rearrange("p (t c) -> p t c", t=2)
                    y = nc.vector.tensor_tensor(area_y[:, rows, :], z[:, :, 0:D], bias[:, 0:1, :].broadcast_to([P, 2, D]), ALU.add)
                    if h:
                        y.then_inc(y_saved, 1)
                    nc.vector.tensor_tensor(base[:, rows, :], z[:, :, D:2 * D], base[:, rows, :], ALU.add)
                    nc.vector.tensor_copy(cs[:, 0, rows], z[:, :, 2 * D + 1])
                    last = nc.vector.tensor_scalar(cs[:, 1, rows], z[:, :, 2 * D], wab[:, 0:1], None, ALU.add)
                last.then_inc(proj_saved, 1)
            dve.wait_ge(proj_saved, GROUPS)
            dve.sem_inc(z_free, 2)
            nc.vector.memset(cs_parts[:, 0, :, 3:6], 1.0)
            nc.vector.memset(cs_parts[:, 1, :, 0:3], 1.0)
            hi = [cs_parts[:, 0, :, 0], cs_parts[:, 1, :, 3]]
            mid = [cs_parts[:, 0, :, 1], cs_parts[:, 1, :, 4]]
            lo = [cs_parts[:, 0, :, 2], cs_parts[:, 1, :, 5]]
            for k in range(2):
                link(nc.vector.tensor_copy(hi[k], cs[:, k, :]))
                link(nc.vector.tensor_tensor(cs_rest[:, k, :], cs[:, k, :], hi[k], ALU.subtract))
                link(nc.vector.tensor_copy(mid[k], cs_rest[:, k, :]))
                last = nc.vector.tensor_tensor(lo[k], cs_rest[:, k, :], mid[k], ALU.subtract)
            last.then_inc(cs_ready, 1)
            dve.wait_ge(zeroed, 2)
            for k in range(4):
                dve.wait_ge(zt_ready, 2 * k + 2)
                last = nc.vector.tensor_copy(z_rows[0:6, k * QC:(k + 1) * QC], tb[1][:, :].bitcast(bf16)[0:6, :])
                last.then_inc(zt_saved, 1)

            with dve.Fori(0, GROUPS) as g:
                for q in range(UNITS):
                    dve.wait_ge(a_loaded[q], g * 16 + 16)
                    first = g * (UNITS * QB) + q * QB

                    def neg_max(t):
                        dve.wait_ge(z_free, first + (2 * t + 4))
                        nc.vector.tensor_scalar(negmax[:, bass.ds(g * GT + t, 1), q], top[:, t, 0:1], top[:, t, 1:2], -1.0,
                                                ALU.max, ALU.mult).then_inc(max_ready, 1)

                    for t in range(GT):
                        dve.wait_ge(p_free, g * (UNITS * GT) + (q * GT + t + 1))
                        for h in range(2):
                            dve.wait_ge(z_ready, first + (2 * t + h + 1))
                            cols = slice(h * ZC, (h + 1) * ZC)
                            dve.sem_inc(passed, 1)
                            nc.vector.tensor_tensor_reduce(out=scores[:, t, cols], in0=area_a[:, q, t, cols], in1=zb[h][:, :],
                                                           scale=1.0, scalar=-3.0e38, op0=ALU.mult, op1=ALU.max,
                                                           accum_out=top[:, t, h:h + 1]).then_inc(z_free, 1)
                        if t:
                            neg_max(t - 1)
                    neg_max(GT - 1)

            dve.wait_ge(unit_read, GROUPS * UNITS)
            dve.wait_ge(y_split, GROUPS)
            for m in reversed(range(4)):
                nc.vector.tensor_tensor(area_y[:, m * QB:(m + 1) * QB, :], acc[m][:, :].rearrange("p (t d) -> p t d", t=QB),
                                        bias[:, 5:6, :].broadcast_to([P, QB, D]), ALU.add).then_inc(acc_free, 1)

            def unpack(p, c, first):
                if not first:
                    dve.wait_ge(v_ready, p * (2 * TILES) + (2 * (1 - c * QB) if c else 0))
                for a in range(2):
                    src = packed[:, bass.ds(p * 2 + a, 1), c * QB:(c + 1) * QB, :].rearrange("p g b i -> p (g b) i")
                    for t in range(GT):
                        last = nc.vector.tensor_scalar(stage[:, a, c * QB:(c + 1) * QB, t, :], src, 1 << t, 14 - t,
                                                       ALU.bitwise_and, ALU.logical_shift_left)
                last.then_inc(staged, 1)

            dve.wait_ge(p_free, GROUPS * UNITS * GT + GT)
            dve.wait_ge(max_ready, GROUPS * UNITS * GT)
            low, total, inverse, rho = (small[:, k, :] for k in range(4))
            link(nc.vector.tensor_reduce(low, negmax[:, :, :], AX, ALU.min))
            nc.vector.tensor_tensor(share[:, :, :], low.unsqueeze(2).broadcast_to([P, TILES, UNITS]), negmax[:, :, :],
                                    ALU.subtract).then_inc(share_in, 1)
            dve.wait_ge(t_free, GROUPS * UNITS * 2 + 2)
            unpack(0, 3, True)
            dve.wait_ge(share_out, 1)
            link(nc.vector.tensor_tensor(share[:, :, :], share[:, :, :], sums[:, :, :], ALU.mult))
            link(nc.vector.tensor_reduce(total, share[:, :, :], AX, ALU.add))
            link(nc.vector.reciprocal(inverse, total))
            link(nc.vector.tensor_tensor(share[:, :, :], share[:, :, :], inverse.unsqueeze(2).broadcast_to([P, TILES, UNITS]), ALU.mult))
            link(nc.vector.tensor_reduce(rho, share[:, :, :], AX, ALU.add))

            mean, var, s0, inv, s1 = ln[:, 0, :], ln[:, 1, :], ln[:, 2, :], ln[:, 3, :], ln[:, 4, :]

            def wide(v):
                return v.unsqueeze(2).broadcast_to([P, QB, D])

            def norm_a(step, y):
                step(nc.vector.tensor_reduce(mean, y, AX, ALU.add))
                step(nc.vector.tensor_scalar(mean, mean, 1.0 / D, None, ALU.mult))
                step(nc.vector.tensor_tensor(y, y, wide(mean), ALU.subtract))
                step(nc.vector.tensor_tensor(tmp_b, y, y, ALU.mult))
                step(nc.vector.tensor_reduce(var, tmp_b, AX, ALU.add))
                nc.vector.tensor_scalar(var, var, 1.0 / D, EPS, ALU.mult, ALU.add).then_inc(var_ready, 1)

            def norm_b(step, y, dst):
                step(nc.vector.reciprocal(inv, s0))
                step(nc.vector.tensor_tensor(s1, var, inv, ALU.mult))
                step(nc.vector.tensor_tensor(s1, s1, s0, ALU.add))
                step(nc.vector.reciprocal(inv, s1))
                step(nc.vector.tensor_scalar(inv, inv, 2.0, None, ALU.mult))
                return nc.vector.tensor_tensor(dst, y, wide(inv), ALU.mult)

            def batch(n):
                m = 3 - n
                rows = slice(m * QB, (m + 1) * QB)
                link(nc.vector.tensor_tensor(tmp_a, area_y[:, rows, :], wide(small[:, 3, rows]), ALU.mult))
                link(nc.vector.tensor_tensor(tmp_a, tmp_a, base[:, rows, :], ALU.add))
                norm_a(link, tmp_a)
                dve.wait_ge(std_ready, n + 1)
                norm_b(link, tmp_a, x1[:, rows, :]).then_inc(x1_ready, 1)

            def split_support(n):
                m = 3 - n
                hi, mid, lo = (parts[:, m * QB:(m + 1) * QB, k * D:(k + 1) * D] for k in range(3))
                dve.wait_ge(s_saved, 2 * n + 2)
                link(nc.vector.tensor_tensor(rest[:, :, :], supp[:, :, :], hi, ALU.subtract))
                link(nc.vector.tensor_copy(mid, rest[:, :, :]))
                nc.vector.tensor_tensor(lo, rest[:, :, :], mid, ALU.subtract).then_inc(s_split, 1)

            dve.wait_ge(acc_free, 4)
            batch(0)
            split_support(0)
            for n in range(1, 4):
                unpack(0, 3 - n, True)
                batch(n)
                split_support(n)

            def take(p, step):
                dve.wait_ge(out_ready, p + 1)
                for a in range(2):
                    dve.wait_ge(w_used, p * (2 * TILES) + (2 * TILES - 1 + a))
                    for h in range(2):
                        nc.vector.tensor_reduce(tmp_a[:, 4 * a + 2 * h:4 * a + 2 * h + 2, :],
                                                acc[2 * a + h][:, 0:6 * D].rearrange("p (t k d) -> p t d k", t=2, k=3),
                                                AX, ALU.add).then_inc(acc_free, 1)

            def finish_a(p, step):
                rows = bass.ds(p * PT, PT) if not isinstance(p, int) else slice(p * PT, (p + 1) * PT)
                dve.wait_ge(acc_free, p * 4 + 8)
                step(nc.vector.tensor_tensor(tmp_a, tmp_a, x1b[:, rows, :], ALU.add))
                norm_a(step, tmp_a)

            def finish_b(p, step):
                rows = bass.ds(p * PT, PT) if not isinstance(p, int) else slice(p * PT, (p + 1) * PT)
                dve.wait_ge(std_ready, p + 5)
                norm_b(step, tmp_a, x1b[:, rows, :]).then_inc(out_ready, 1)

            dve.wait_ge(x1b_ready, 4)
            dve.wait_ge(x1_ready, 4)
            dve.sem_inc(out_ready, 1)
            before = count[0]
            with dve.Fori(1, PAIRS) as p:
                here = [0]

                def step(ins):
                    here[0] += 1
                    ins.then_inc(dve_done, 1)
                    dve.wait_ge(dve_done, p * 11 + (before - 11 + here[0]))

                for c in (3, 2, 1):
                    unpack(p, c, False)
                take(p - 1, step)
                finish_a(p - 1, step)
                unpack(p, 0, False)
                finish_b(p - 1, step)
                assert here[0] == 11
            count[0] += 11 * (PAIRS - 1)
            take(PAIRS - 1, link)
            finish_a(PAIRS - 1, link)
            finish_b(PAIRS - 1, link)

        @block.tensor
        def _(pe):
            mm = nc.tensor.matmul
            pe.wait_ge(consts, 1)
            pe.wait_ge(xr_loaded, 32)

            def transpose_xr(k):
                if k >= 2:
                    pe.wait_ge(xrt_saved, k - 1)
                for j in range(GT):
                    last = nc.tensor.transpose(tb[k % 2][:, j * P:(j + 1) * P], xr[:, k * GT + j, :], identf[:, :])
                last.then_inc(xrt_ready, 1)

            transpose_xr(0)
            pe.wait_ge(w_loaded, 16 * 13)
            for k in range(GROUPS):
                if k + 1 < GROUPS:
                    transpose_xr(k + 1)
                pe.wait_ge(xrt_saved, k + 1)
                if k:
                    pe.wait_ge(proj_saved, k)
                for j in range(GT):
                    t = k * GT + j
                    lhs = xrt[:, k % 2, j * P:(j + 1) * P]
                    mm(zb[j // 2][:, (j % 2) * WCOLS:(j % 2 + 1) * WCOLS], lhs, w_all[:, :], start=j % 2 == 0, stop=True, skip_group_check=True)
                    last = mm(acc[t // QB][:, (t % QB) * D:(t % QB + 1) * D], lhs, w_agg[:, :], start=t % QB == 0, stop=True, skip_group_check=True)
                last.then_inc(proj_ready, 1)
            pe.wait_ge(cs_ready, 1)
            for k in range(4):
                if k:
                    pe.wait_ge(zt_saved, 2 * k)
                for i in range(2):
                    for j in range(QB):
                        last = nc.tensor.transpose(tb[i][:, :].bitcast(bf16)[0:6, j * P:(j + 1) * P], cs_parts[:, i, k * QB + j, :], ident[:, 0, :])
                    last.then_inc(zt_ready, 1)
            pe.wait_ge(zt_saved, 8)
            pe.wait_ge(proj_saved, GROUPS)

            with pe.Fori(0, GROUPS) as g:
                pe.wait_ge(y_split, g + 1)
                for q in range(UNITS):
                    pe.wait_ge(a_loaded[q], g * 16 + 16)
                    for b in range(QB):
                        t, h = b // 2, b % 2
                        pe.wait_ge(z_free, g * (UNITS * QB) + (q * QB + b + 1))
                        mm(zb[h][:, :], z_rows[:, bass.ds(g * GW + t * P, P)], z_cols[:, q * QC + h * ZC:q * QC + (h + 1) * ZC],
                           start=True, stop=True).then_inc(z_ready, 1)
                        s = b // 4
                        if b % 4 == 0:
                            pe.wait_ge(t_free, g * (2 * UNITS) + (2 * q + s + 1))
                        for t in range(GT):
                            lhs = block_t(q, t, b)
                            last = mm(tb[s][:, (b % 4) * P:(b % 4 + 1) * P], lhs, ident[:, t, :],
                                      start=b % 4 == 0 and t == 0, stop=True, skip_group_check=True)
                            if b % 4 == 3 and t == GT - 1:
                                last.then_inc(t_ready, 1)
                            for k in range(3):
                                last = mm(acc[q][:, b * D:(b + 1) * D], lhs,
                                          parts[:, bass.ds(g * GT + t, 1), k * D:(k + 1) * D].rearrange("p g d -> p (g d)"),
                                          start=False, stop=True, skip_group_check=True)
                    last.then_inc(unit_read, 1)

            def transpose_x1(n):
                m = 3 - n
                pe.wait_ge(x1_ready, n + 1)
                if n:
                    pe.wait_ge(s_saved, 2 * n)
                else:
                    pe.wait_ge(t_free, GROUPS * UNITS * 2 + 2)
                for s in range(2):
                    for j in range(4):
                        last = nc.tensor.transpose(tb[s][0:D, j * P:(j + 1) * P], x1[:, m * QB + s * 4 + j, :], identf[:, :])
                    last.then_inc(x1t_ready, 1)

            def support(n):
                pe.wait_ge(x1t_saved, 2 * n + 2)
                for j in range(QB):
                    last = mm(tb[0][:, j * D:(j + 1) * D], x1t[:, j * P:(j + 1) * P], w_l1[:, :], start=j == 0, stop=True, skip_group_check=True)
                last.then_inc(s_ready, 1)

            def count_in(b, a):
                mm(zb[a][:, :], upto[:, :], stage_bf[:, a, b, :], start=b == TILES - 1, stop=True, skip_group_check=True).then_inc(v_ready, 1)

            def pair(p, first):
                pe.wait_ge(staged, p * 4 + 1)
                for a in range(2):
                    count_in(TILES - 1, a)
                for b in reversed(range(TILES)):
                    if b % QB == 7 and first:
                        pe.wait_ge(s_split, 4 - b // QB)
                    for a in range(2):
                        n = 2 * (TILES - 1 - b) + a
                        pe.wait_ge(w_ready, p * (2 * TILES) + (n + 1))
                        if b:
                            last = mm(zb[a][:, :], beyond[:, :], stage_bf[:, a, b, :], start=False, stop=True, skip_group_check=True)
                            if b % QB == 0 and not a:
                                pe.wait_ge(staged, p * 4 + (4 - b // QB + 1))
                            count_in(b - 1, a)
                        if b == TILES - 1:
                            pe.wait_ge(acc_free, p * 4 + (2 * a + 2) if not first else 4)
                        for t in range(GT):
                            last = mm(acc[2 * a + t // 2][:, (t % 2) * 3 * D:(t % 2 + 1) * 3 * D],
                                      weights_bf[:, a, b % 2, t * P:(t + 1) * P], parts[:, b, :],
                                      start=b == TILES - 1 and t % 2 == 0, stop=True, skip_group_check=True)
                        last.then_inc(w_used, 1)
                    if first and b >= QB:
                        n = 4 - b // QB
                        if b % QB == 6:
                            transpose_x1(n)
                        if b % QB == 5:
                            support(n)

            pe.wait_ge(unit_read, GROUPS * UNITS)
            transpose_x1(0)
            support(0)
            pair(0, True)
            with pe.Fori(1, PAIRS) as p:
                pair(p, False)


_ORDER = ["x", "adj", "L0_gnn_relationship_features", "L0_gnn_W_obj", "L0_gnn_b_obj", "L0_gnn_W_nobj", "L0_gnn_b_nobj",
          "L0_gnn_W_rel", "L0_gnn_b_rel", "L0_gnn_W_skip", "L0_gnn_b_skip", "L0_gnn_Wa_w", "L0_gnn_Wa_b",
          "L1_gnn_weight", "L1_gnn_bias"]


def kernel(**inputs):
    import numpy as np
    import concourse.bacc as bacc
    from concourse.bass_utils import run_bass_kernel_spmd

    nc = bacc.Bacc("TRN2", target_bir_lowering=False, num_devices=1)
    arrays, args = {}, []
    for name in _ORDER:
        a = np.ascontiguousarray(inputs[name])
        arrays[f"in_{name}"] = a
        args.append(nc.dram_tensor(f"in_{name}", a.shape, mybir.dt.from_np(a.dtype), kind="ExternalInput").ap())
    out = nc.dram_tensor("out", (N, D), mybir.dt.float32, kind="ExternalOutput").ap()
    build(nc, *args, out)
    r = run_bass_kernel_spmd(nc, [arrays], core_ids=[0])
    return r.results[0]["out"]
```

```python
from contextlib import ExitStack

import concourse.bass as bass
from concourse import mybir
from concourse.alu_op_type import AluOpType as ALU

N, D, P = 4096, 64, 128
TILES = N // P
GT = 4
GROUPS = TILES // GT
QB = 8
UNITS = TILES // QB
QC = QB * P
ZC = 512
GW = GT * P
PAIRS = GROUPS // 2
PT = 2 * GT
RING = 4
LEAD = RING - 1
BT = 4
BATCHES = TILES // BT
MAX_NEIGH = 100
EPS = 1e-5
STEP = 128.0
OWN = 16384.0
SHIFT = 2.0 ** (127 - MAX_NEIGH)
ON = 2.0
WCOLS = 2 * D + 2


def build(nc, x, adj, rel, W_obj, b_obj, W_nobj, b_nobj, W_rel, b_rel, W_skip, b_skip, Wa_w, Wa_b,
          W_l1, b_l1, out):
    fp32, bf16, u16 = mybir.dt.float32, mybir.dt.bfloat16, mybir.dt.uint16
    ACT = mybir.ActivationFunctionType
    AX = mybir.AxisListType.X
    es = ExitStack()
    with es:
        def sb(name, shape, dt):
            return es.enter_context(nc.sbuf_tensor(name, shape, dt))

        def sem(name):
            return es.enter_context(nc.semaphore(name))

        packed = sb("packed", [P, GROUPS, TILES, P], u16)
        area_a = sb("area_a", [P, UNITS, GT, QC], fp32)
        stage = area_a[:, :, :, :].rearrange("p u t c -> p (u t c)").bitcast(u16).rearrange(
            "p (u a b t c) -> p u a b t c", u=UNITS, a=2, b=QB, t=GT)
        stage_bf = area_a[:, :, :, :].rearrange("p u t c -> p (u t c)").bitcast(bf16).rearrange(
            "p (u a b i) -> p u a b i", u=UNITS, a=2, b=QB)
        area_p = sb("area_p", [P, GT * QC], fp32)
        scores = area_p[:, :].rearrange("p (t c) -> p t c", t=GT)
        xr = area_p[:, :].rearrange("p (t c) -> p t c", t=TILES)
        x1 = area_p[:, 0:TILES * D].rearrange("p (t d) -> p t d", t=TILES)
        x1b = area_p[:, TILES * D:2 * TILES * D].rearrange("p (t d) -> p t d", t=TILES)
        area_y = sb("area_y", [P, TILES, D], fp32)
        base = sb("base", [P, TILES, D], fp32)
        parts = sb("parts", [P, TILES, 3 * D], bf16)
        area_z = sb("area_z", [P, 2, N], bf16)
        z_cols, z_rows = area_z[:, 0, :], area_z[:, 1, :]
        weights = area_z[:, 0, 0:2 * RING * GW].bitcast(u16).rearrange("p (a s i) -> p a s i", a=2, s=RING)
        weights_bf = area_z[:, 0, 0:2 * RING * GW].rearrange("p (a s i) -> p a s i", a=2, s=RING)
        x1t = area_z[0:D, 1, 0:2 * 2 * GW].bitcast(fp32).rearrange("p (h i) -> p h i", h=2)
        xrt = sb("xrt", [P, 2, GW], fp32)
        tmp_a = xrt[:, 0, :].rearrange("p (t d) -> p t d", t=QB)
        tmp_b = xrt[:, 1, :].rearrange("p (t d) -> p t d", t=QB)
        supp = sb("supp", [P, 2, BT, D], fp32)
        rest = sb("rest", [P, BT, D], fp32)
        rest_y = sb("rest_y", [P, GT, D], fp32)
        identf = sb("identf", [P, P], fp32)
        ident = sb("ident", [P, GT, P], bf16)
        upto = sb("upto", [P, P], bf16)
        beyond = sb("beyond", [P, P], bf16)
        w_all = sb("w_all", [P, WCOLS], fp32)
        w_agg = sb("w_agg", [P, D], fp32)
        w_l1 = sb("w_l1", [D, D], fp32)
        bias = sb("bias", [P, 6, D], fp32)
        wab = sb("wab", [P, 1], fp32)
        floor = sb("floor", [P, 1], fp32)
        cs = sb("cs", [P, 2, TILES], fp32)
        cs_rest = sb("cs_rest", [P, 2, TILES], fp32)
        cs_parts = sb("cs_parts", [P, TILES, 18], bf16)
        top = sb("top", [P, GT, 2], fp32)
        negmax = sb("negmax", [P, TILES, UNITS], fp32)
        sums = sb("sums", [P, TILES, UNITS], fp32)
        small = sb("small", [P, 8, TILES], fp32)
        share = sb("share", [P, TILES, UNITS], fp32)
        ln = sb("ln", [P, 8, QB], fp32)
        root_warm = sb("root_warm", [P, 1], fp32)

        acc = [es.enter_context(nc.psum_tensor(f"acc{i}", [P, 512], fp32)) for i in range(4)]
        zb = [es.enter_context(nc.psum_tensor(f"zb{i}", [P, 512], fp32)) for i in range(2)]
        tb = [es.enter_context(nc.psum_tensor(f"tb{i}", [P, 512], fp32)) for i in range(2)]

        xr_loaded, w_loaded, zeroed = sem("xr_loaded"), sem("w_loaded"), sem("zeroed")
        ident_ready, consts = sem("ident_ready"), sem("consts")
        a_loaded = [sem(f"a_loaded{q}") for q in range(UNITS)]
        xrt_ready, xrt_saved, proj_ready, proj_saved = sem("xrt_ready"), sem("xrt_saved"), sem("proj_ready"), sem("proj_saved")
        skip_ready, cs_ready, zt_ready = sem("skip_ready"), sem("cs_ready"), sem("zt_ready")
        zc_saved, zr_saved = sem("zc_saved"), sem("zr_saved")
        y_saved, y_split = sem("y_saved"), sem("y_split")
        z_ready, z_free = sem("z_ready"), sem("z_free")
        t_ready, t_free = sem("t_ready"), sem("t_free")
        unit_read = sem("unit_read")
        max_ready, p_free = sem("max_ready"), sem("p_free")
        share_in, share_out = sem("share_in"), sem("share_out")
        var_ready, std_ready = sem("var_ready"), sem("std_ready")
        x1_ready, x1t_ready, x1t_saved = sem("x1_ready"), sem("x1t_ready"), sem("x1t_saved")
        s_ready, s_saved, s_split = sem("s_ready"), sem("s_saved"), sem("s_split")
        x1b_ready = sem("x1b_ready")
        staged = sem("staged")
        v_ready, w_ready, w_used = sem("v_ready"), sem("w_ready"), sem("w_used")
        acc_free = sem("acc_free")
        out_ready, out_done = sem("out_ready"), sem("out_done")
        dve_done, pool_done = sem("dve_done"), sem("pool_done")
        passed, passed_pool = sem("passed"), sem("passed_pool")

        adj_v = adj.rearrange("(g t p) c -> p g t c", t=GT, p=P)
        x_v = x.rearrange("(t p) d -> p t d", p=P)
        r_v = rel.rearrange("(t p) d -> p t d", p=P)
        out_v = out.rearrange("(t p) d -> p t d", p=P)

        def block_t(q, t, b):
            v = area_a[:, q, t, b * P:(b + 1) * P].bitcast(bf16)
            return v.rearrange("p (c h) -> p c h", h=2)[:, :, 1]

        block = es.enter_context(nc.Block())

        @block.sync
        def _(sp):
            sp.dma_start(xr[:, :, 0:D], x_v).then_inc(xr_loaded, 16)
            sp.dma_start(xr[:, :, D:2 * D], r_v).then_inc(xr_loaded, 16)
            sp.wait_ge(w_loaded, 16 * 13)
            for q in range(UNITS):
                sp.dma_start(area_a[:, q, :, :], adj_v[:, 0, :, q * QC:(q + 1) * QC]).then_inc(a_loaded[q], 16)
            with sp.Fori(1, GROUPS) as g:
                for q in range(UNITS):
                    sp.wait_ge(unit_read, g * UNITS + (q + 1 - UNITS))
                    sp.wait_ge(z_free, (g * UNITS + (q + 1 - UNITS)) * QB + 2)
                    sp.dma_start(area_a[:, q, :, :], adj_v[:, bass.ds(g, 1), :, q * QC:(q + 1) * QC].rearrange("p g t c -> p (g t) c")).then_inc(a_loaded[q], 16)
            with sp.Fori(0, PAIRS) as g:
                sp.wait_ge(out_ready, g + 2)
                sp.dma_start(out_v[:, bass.ds(g * PT, PT), :], x1b[:, bass.ds(g * PT, PT), :]).then_inc(out_done, 16)
            sp.wait_ge(out_done, 16 * PAIRS)

        @block.gpsimd
        def _(pool):
            count = [0]

            def link(ins):
                count[0] += 1
                ins.then_inc(pool_done, 1)
                pool.wait_ge(pool_done, count[0])

            def diagonal(tile, fill):
                return nc.gpsimd.affine_select(out=tile, in_=tile, compare_op=ALU.not_equal, fill=fill, base=0,
                                               pattern=[[-1, P]], channel_multiplier=1)

            link(nc.gpsimd.memset(identf[:], 0.0))
            diagonal(identf[:, :], 1.0).then_inc(ident_ready, 1)
            pool.wait_ge(w_loaded, 16 * 13)
            pool.wait_ge(xr_loaded, 32)
            nc.gpsimd.tensor_tensor(bias[:, 5, :], bias[:, 2, :], bias[:, 3, :], ALU.add)
            nc.gpsimd.tensor_tensor(base[:, :, :], xr[:, :, 0:D], bias[:, 1:2, :].broadcast_to([P, TILES, D]), ALU.add).then_inc(skip_ready, 1)
            for t in range(GT):
                nc.gpsimd.memset(ident[:, t, :], 0.0)
            nc.gpsimd.memset(floor[:], STEP * (MAX_NEIGH + 1) - OWN)
            nc.gpsimd.memset(upto[:], -STEP / ON)
            link(nc.gpsimd.memset(beyond[:], -STEP / ON))
            for t in range(GT):
                diagonal(ident[:, t, :], 2.0 ** t)
            nc.gpsimd.affine_select(out=upto[:, :], in_=upto[:, :], compare_op=ALU.is_ge, fill=0.0, base=0,
                                    pattern=[[-1, P]], channel_multiplier=1)
            link(nc.gpsimd.affine_select(out=beyond[:, :], in_=beyond[:, :], compare_op=ALU.is_ge, fill=0.0, base=0,
                                         pattern=[[1, P]], channel_multiplier=-1))
            diagonal(upto[:, :], (OWN - STEP) / ON)
            diagonal(beyond[:, :], -OWN / ON).then_inc(consts, 1)
            done = count[0]
            with pool.Fori(0, GROUPS) as g:
                y = area_y[:, bass.ds(g * GT, GT), :]
                hi, mid, lo = (parts[:, bass.ds(g * GT, GT), k * D:(k + 1) * D] for k in range(3))
                pool.wait_ge(y_saved, g + 1)
                pool.sem_inc(passed_pool, 1)
                nc.gpsimd.tensor_copy(hi, y).then_inc(pool_done, 1)
                pool.wait_ge(pool_done, g * 4 + (done + 1))
                pool.sem_inc(passed_pool, 1)
                nc.gpsimd.tensor_tensor(rest_y[:, :, :], y, hi, ALU.subtract).then_inc(pool_done, 1)
                pool.wait_ge(pool_done, g * 4 + (done + 2))
                pool.sem_inc(passed_pool, 1)
                nc.gpsimd.tensor_copy(mid, rest_y[:, :, :]).then_inc(pool_done, 1)
                pool.wait_ge(pool_done, g * 4 + (done + 3))
                pool.sem_inc(passed_pool, 1)
                nc.gpsimd.tensor_tensor(lo, rest_y[:, :, :], mid, ALU.subtract).then_inc(y_split, 1)
                pool.wait_ge(y_split, g + 1)
                pool.sem_inc(passed_pool, 1)
                nc.gpsimd.tensor_copy(rest_y[:, :, 0:1], rest_y[:, :, 0:1]).then_inc(pool_done, 1)
            for n in range(BATCHES):
                pool.wait_ge(x1_ready, n + 1)
                rows = slice(TILES - (n + 1) * BT, TILES - n * BT)
                nc.gpsimd.tensor_tensor(x1b[:, rows, :], x1[:, rows, :], bias[:, 4:5, :].broadcast_to([P, BT, D]), ALU.add).then_inc(x1b_ready, 1)

        @block.scalar
        def _(act):
            act.dma_start(bias[:, 0, :], b_nobj.partition_broadcast(P)).then_inc(w_loaded, 16)
            act.dma_start(bias[:, 1, :], b_skip.partition_broadcast(P)).then_inc(w_loaded, 16)
            act.dma_start(bias[:, 2, :], b_obj.partition_broadcast(P)).then_inc(w_loaded, 16)
            act.dma_start(bias[:, 3, :], b_rel.partition_broadcast(P)).then_inc(w_loaded, 16)
            act.dma_start(bias[:, 4, :], b_l1.partition_broadcast(P)).then_inc(w_loaded, 16)
            act.dma_start(wab[:, :], Wa_b.partition_broadcast(P)).then_inc(w_loaded, 16)
            act.dma_start(w_agg[0:D, :], W_obj).then_inc(w_loaded, 16)
            act.dma_start(w_agg[D:P, :], W_rel).then_inc(w_loaded, 16)
            act.dma_start(w_l1[:, :], W_l1).then_inc(w_loaded, 16)
            act.wait_ge(zeroed, 1)
            act.dma_start(w_all[0:D, 0:D], W_nobj).then_inc(w_loaded, 16)
            act.dma_start(w_all[0:D, D:2 * D], W_skip).then_inc(w_loaded, 16)
            act.dma_start(w_all[0:D, 2 * D:2 * D + 1], Wa_w[0:D, :]).then_inc(w_loaded, 16)
            act.dma_start(w_all[D:P, 2 * D + 1:2 * D + 2], Wa_w[D:2 * D, :]).then_inc(w_loaded, 16)
            for k in range(GROUPS):
                act.wait_ge(xrt_ready, k + 1)
                if k >= 2:
                    act.wait_ge(proj_ready, k - 1)
                nc.scalar.activation(xrt[:, k % 2, :], tb[k % 2][:, :], ACT.Copy).then_inc(xrt_saved, 1)
            act.wait_ge(zeroed, 2)
            for k in range(4):
                act.wait_ge(zt_ready, 2 * k + 1)
                nc.scalar.activation(z_cols[0:6, k * QC:(k + 1) * QC], [tb, zb][k % 2][0][:, :].bitcast(bf16)[0:6, :], ACT.Copy).then_inc(zc_saved, 1)
            act.wait_ge(zc_saved, 4)
            act.wait_ge(zr_saved, 4)
            act.sem_inc(t_free, 2)
            act.sem_inc(p_free, GT)
            with act.Fori(0, GROUPS) as g:
                for q in range(UNITS):

                    def exps(t):
                        act.wait_ge(max_ready, g * (UNITS * GT) + (q * GT + t + 1))
                        nc.scalar.activation(scores[:, t, :], scores[:, t, :], ACT.Exp,
                                             bias=negmax[:, bass.ds(g * GT + t, 1), q],
                                             accum_out=sums[:, bass.ds(g * GT + t, 1), q]).then_inc(p_free, 1)

                    def save_transpose(s):
                        act.wait_ge(t_ready, g * (2 * UNITS) + (2 * q + s + 1))
                        nc.scalar.activation(
                            packed[:, bass.ds(g, 1), q * QB + s * 4:q * QB + s * 4 + 4, :].rearrange("p g b i -> p (g b i)"),
                            tb[s][:, :], ACT.Copy).then_inc(t_free, 1)

                    exps(0)
                    save_transpose(0)
                    exps(1)
                    exps(2)
                    save_transpose(1)
                    exps(3)
            act.wait_ge(share_in, 1)
            nc.scalar.activation(share[:, :, :], share[:, :, :], ACT.Exp).then_inc(share_out, 1)
            nc.scalar.activation(root_warm[:, :], floor[:, :], ACT.Sqrt, scale=-1.0)

            def std(n):
                act.wait_ge(var_ready, n + 1)
                nc.scalar.activation(ln[:, 2, 0:BT], ln[:, 1, 0:BT], ACT.Sqrt).then_inc(std_ready, 1)

            def std_pair(p):
                act.wait_ge(var_ready, p + (BATCHES + 1))
                nc.scalar.activation(ln[:, 2, :], ln[:, 1, :], ACT.Sqrt).then_inc(std_ready, 1)

            def save_x1t(n):
                act.wait_ge(x1t_ready, n + 1)
                if n >= 2:
                    act.wait_ge(s_ready, n - 1)
                nc.scalar.activation(x1t[:, n % 2, :], tb[0][0:D, :], ACT.Copy).then_inc(x1t_saved, 1)

            def save_support(n):
                act.wait_ge(s_ready, n + 1)
                if n >= 2:
                    act.wait_ge(s_split, n - 1)
                nc.scalar.activation(supp[:, n % 2, :, :].rearrange("p t d -> p (t d)"), tb[1][:, 0:BT * D], ACT.Copy, scale=SHIFT).then_inc(s_saved, 1)
                act.wait_ge(s_saved, 2 * n + 1)
                nc.scalar.activation(parts[:, TILES - (n + 1) * BT:TILES - n * BT, 0:D], supp[:, n % 2, :, :], ACT.Copy).then_inc(s_saved, 1)

            def weigh(p, b, first):
                for a in range(2):
                    n = 2 * (TILES - 1 - b) + a
                    act.wait_ge(v_ready, p * (2 * TILES) + (n + 1))
                    if not (first and n < 2 * RING):
                        act.wait_ge(w_used, p * (2 * TILES) + (n + 1 - 2 * RING))
                    nc.scalar.activation(weights[:, a, b % RING, :], zb[a][:, :], ACT.Relu, bias=floor[:, 0:1]).then_inc(w_ready, 1)

            for b in reversed(range(TILES - LEAD, TILES)):
                weigh(0, b, True)
            std(0)
            save_x1t(0)
            save_support(0)
            std(1)
            for b in reversed(range(TILES - LEAD)):
                n = BATCHES - (b + LEAD) // BT
                at = (b + LEAD) % BT
                if n < BATCHES and at == 2:
                    save_x1t(n)
                if n < BATCHES and at == 0:
                    save_support(n)
                    if n + 1 < BATCHES:
                        std(n + 1)
                weigh(0, b, True)
            with act.Fori(1, PAIRS) as p:
                for b in reversed(range(TILES)):
                    weigh(p, b, False)
                    if b == TILES - 4 - LEAD:
                        std_pair(p - 1)
            std_pair(PAIRS - 1)

        @block.vector
        def _(dve):
            count = [0]

            def link(ins):
                count[0] += 1
                ins.then_inc(dve_done, 1)
                dve.wait_ge(dve_done, count[0])

            nc.vector.memset(w_all[:], 0.0).then_inc(zeroed, 1)
            nc.vector.memset(cs_parts[:, :, 3:9], 1.0)
            nc.vector.memset(area_z[:, :, :], 0.0).then_inc(zeroed, 1)
            dve.wait_ge(w_loaded, 16 * 13)
            dve.wait_ge(skip_ready, 1)
            for k in range(GROUPS):
                for h in range(2):
                    dve.wait_ge(proj_ready, 2 * k + h + 1)
                    rows = slice(k * GT + 2 * h, k * GT + 2 * h + 2)
                    z = zb[h][:, 0:2 * WCOLS].rearrange("p (t c) -> p t c", t=2)
                    y = nc.vector.tensor_tensor(area_y[:, rows, :], z[:, :, 0:D], bias[:, 0:1, :].broadcast_to([P, 2, D]), ALU.add)
                    if h:
                        y.then_inc(y_saved, 1)
                    nc.vector.tensor_tensor(base[:, rows, :], z[:, :, D:2 * D], base[:, rows, :], ALU.add)
                    nc.vector.tensor_copy(cs[:, 0, rows], z[:, :, 2 * D + 1])
                    nc.vector.tensor_scalar(cs[:, 1, rows], z[:, :, 2 * D], wab[:, 0:1], None, ALU.add).then_inc(proj_saved, 1)
            dve.wait_ge(proj_saved, 2 * GROUPS)
            hi, mid, lo = (cs_parts[:, :, :].rearrange("p t (k c) -> p k t c", k=2)[:, :, :, k] for k in range(3))
            link(nc.vector.tensor_copy(hi, cs[:, :, :]))
            link(nc.vector.tensor_tensor(cs_rest[:, :, :], cs[:, :, :], hi, ALU.subtract))
            link(nc.vector.tensor_copy(mid, cs_rest[:, :, :]))
            nc.vector.tensor_tensor(lo, cs_rest[:, :, :], mid, ALU.subtract).then_inc(cs_ready, 1)
            dve.wait_ge(zeroed, 2)
            for k in range(4):
                dve.wait_ge(zt_ready, 2 * k + 2)
                nc.vector.tensor_copy(z_rows[0:6, k * QC:(k + 1) * QC], [tb, zb][k % 2][1][:, :].bitcast(bf16)[0:6, :]).then_inc(zr_saved, 1)
            dve.wait_ge(zc_saved, 4)
            dve.wait_ge(zr_saved, 4)
            dve.sem_inc(z_free, 2)

            with dve.Fori(0, GROUPS) as g:
                for q in range(UNITS):
                    dve.wait_ge(a_loaded[q], g * 16 + 16)
                    first = g * (UNITS * QB) + q * QB

                    def neg_max(t):
                        dve.wait_ge(z_free, first + (2 * t + 4))
                        nc.vector.tensor_scalar(negmax[:, bass.ds(g * GT + t, 1), q], top[:, t, 0:1], top[:, t, 1:2], -1.0,
                                                ALU.max, ALU.mult).then_inc(max_ready, 1)

                    for t in range(GT):
                        dve.wait_ge(p_free, g * (UNITS * GT) + (q * GT + t + 1))
                        for h in range(2):
                            dve.wait_ge(z_ready, first + (2 * t + h + 1))
                            cols = slice(h * ZC, (h + 1) * ZC)
                            dve.sem_inc(passed, 1)
                            nc.vector.tensor_tensor_reduce(out=scores[:, t, cols], in0=area_a[:, q, t, cols], in1=zb[h][:, :],
                                                           scale=1.0, scalar=-3.0e38, op0=ALU.mult, op1=ALU.max,
                                                           accum_out=top[:, t, h:h + 1]).then_inc(z_free, 1)
                        if t:
                            neg_max(t - 1)
                    neg_max(GT - 1)

            def unpack(p, c, first):
                if not first:
                    dve.wait_ge(v_ready, p * (2 * TILES) + (2 * (1 - c * QB) if c else 0))
                for a in range(2):
                    src = packed[:, bass.ds(p * 2 + a, 1), c * QB:(c + 1) * QB, :].rearrange("p g b i -> p (g b) i")
                    for t in range(GT):
                        last = nc.vector.tensor_scalar(stage[:, UNITS - 1 - c, a, :, t, :], src, 1 << t, 14 - t,
                                                       ALU.bitwise_and, ALU.logical_shift_left)
                last.then_inc(staged, 1)

            dve.wait_ge(unit_read, GROUPS * UNITS - UNITS + 1)
            dve.wait_ge(z_free, GROUPS * UNITS * QB + 2)
            dve.wait_ge(t_free, (GROUPS - 1) * UNITS * 2 + 2)
            unpack(0, 3, True)

            dve.wait_ge(p_free, GROUPS * UNITS * GT + GT)
            dve.wait_ge(max_ready, GROUPS * UNITS * GT)
            low, total, inverse, rho = (small[:, k, :] for k in range(4))
            link(nc.vector.tensor_reduce(low, negmax[:, :, :], AX, ALU.min))
            nc.vector.tensor_tensor(share[:, :, :], low.unsqueeze(2).broadcast_to([P, TILES, UNITS]), negmax[:, :, :],
                                    ALU.subtract).then_inc(share_in, 1)
            dve.wait_ge(unit_read, GROUPS * UNITS)
            dve.wait_ge(y_split, GROUPS)

            def save_aggregate(m):
                nc.vector.tensor_tensor(area_y[:, m * QB:(m + 1) * QB, :], acc[m][:, :].rearrange("p (t d) -> p t d", t=QB),
                                        bias[:, 5:6, :].broadcast_to([P, QB, D]), ALU.add).then_inc(acc_free, 1)

            save_aggregate(3)
            dve.wait_ge(share_out, 1)
            link(nc.vector.tensor_tensor(share[:, :, :], share[:, :, :], sums[:, :, :], ALU.mult))
            link(nc.vector.tensor_reduce(total, share[:, :, :], AX, ALU.add))
            link(nc.vector.reciprocal(inverse, total))
            link(nc.vector.tensor_tensor(share[:, :, :], share[:, :, :], inverse.unsqueeze(2).broadcast_to([P, TILES, UNITS]), ALU.mult))
            link(nc.vector.tensor_reduce(rho, share[:, :, :], AX, ALU.add))

            def norm_a(step, y, w):
                mean, var, square = ln[:, 0, 0:w], ln[:, 1, 0:w], tmp_b[:, 0:w, :]
                step(nc.vector.tensor_reduce(mean, y, AX, ALU.add))
                step(nc.vector.tensor_scalar(mean, mean, 1.0 / D, None, ALU.mult))
                step(nc.vector.tensor_tensor(y, y, mean.unsqueeze(2).broadcast_to([P, w, D]), ALU.subtract))
                step(nc.vector.tensor_tensor(square, y, y, ALU.mult))
                step(nc.vector.tensor_reduce(var, square, AX, ALU.add))
                nc.vector.tensor_scalar(var, var, 1.0 / D, EPS, ALU.mult, ALU.add).then_inc(var_ready, 1)

            def norm_b(step, y, dst, w):
                var, root, inv, twice = (ln[:, k, 0:w] for k in range(1, 5))
                step(nc.vector.reciprocal(inv, root))
                step(nc.vector.tensor_tensor(twice, var, inv, ALU.mult))
                step(nc.vector.tensor_tensor(twice, twice, root, ALU.add))
                step(nc.vector.reciprocal(inv, twice))
                step(nc.vector.tensor_scalar(inv, inv, 2.0, None, ALU.mult))
                return nc.vector.tensor_tensor(dst, y, inv.unsqueeze(2).broadcast_to([P, w, D]), ALU.mult)

            def batch_rows(n):
                return slice(TILES - (n + 1) * BT, TILES - n * BT)

            def batch_a(n):
                y = tmp_a[:, 0:BT, :]
                dve.wait_ge(acc_free, 1 + n // 2)
                if n:
                    dve.wait_ge(x1_ready, n)
                link(nc.vector.tensor_tensor(y, area_y[:, batch_rows(n), :], rho[:, batch_rows(n)].unsqueeze(2).broadcast_to([P, BT, D]), ALU.mult))
                link(nc.vector.tensor_tensor(y, y, base[:, batch_rows(n), :], ALU.add))
                norm_a(link, y, BT)

            def batch_b(n):
                dve.wait_ge(std_ready, n + 1)
                norm_b(link, tmp_a[:, 0:BT, :], x1[:, batch_rows(n), :], BT).then_inc(x1_ready, 1)

            def split_support(n):
                hi, mid, lo = (parts[:, batch_rows(n), k * D:(k + 1) * D] for k in range(3))
                dve.wait_ge(s_saved, 2 * n + 2)
                link(nc.vector.tensor_tensor(rest[:, :, :], supp[:, n % 2, :, :], hi, ALU.subtract))
                link(nc.vector.tensor_copy(mid, rest[:, :, :]))
                link(nc.vector.tensor_tensor(lo, rest[:, :, :], mid, ALU.subtract))
                dve.sem_inc(s_split, 1)

            batch_a(0)
            batch_b(0)
            save_aggregate(2)
            save_aggregate(1)
            save_aggregate(0)
            batch_a(1)
            split_support(0)
            batch_b(1)
            unpack(0, 2, True)
            for n in range(2, BATCHES):
                batch_a(n)
                split_support(n - 1)
                batch_b(n)
                if n == 3:
                    unpack(0, 1, True)
                if n == 5:
                    unpack(0, 0, True)
            split_support(BATCHES - 1)

            def take(p, step):
                dve.wait_ge(out_ready, p + 1)
                for a in range(2):
                    dve.wait_ge(w_used, p * (2 * TILES) + (2 * TILES - 1 + a))
                    for h in range(2):
                        nc.vector.tensor_reduce(tmp_a[:, 4 * a + 2 * h:4 * a + 2 * h + 2, :],
                                                acc[2 * a + h][:, 0:6 * D].rearrange("p (t k d) -> p t d k", t=2, k=3),
                                                AX, ALU.add).then_inc(acc_free, 1)

            def finish_a(p, step):
                rows = bass.ds(p * PT, PT) if not isinstance(p, int) else slice(p * PT, (p + 1) * PT)
                dve.wait_ge(acc_free, p * 4 + 8)
                step(nc.vector.tensor_tensor(tmp_a, tmp_a, x1b[:, rows, :], ALU.add))
                norm_a(step, tmp_a, PT)

            def finish_b(p, step):
                rows = bass.ds(p * PT, PT) if not isinstance(p, int) else slice(p * PT, (p + 1) * PT)
                dve.wait_ge(std_ready, p + (BATCHES + 1))
                norm_b(step, tmp_a, x1b[:, rows, :], PT).then_inc(out_ready, 1)

            dve.wait_ge(x1b_ready, BATCHES)
            dve.wait_ge(x1_ready, BATCHES)
            dve.sem_inc(out_ready, 1)
            before = count[0]
            with dve.Fori(1, PAIRS) as p:
                here = [0]

                def step(ins):
                    here[0] += 1
                    ins.then_inc(dve_done, 1)
                    dve.wait_ge(dve_done, p * 11 + (before - 11 + here[0]))

                for c in (3, 2, 1):
                    unpack(p, c, False)
                take(p - 1, step)
                finish_a(p - 1, step)
                unpack(p, 0, False)
                finish_b(p - 1, step)
                assert here[0] == 11
            count[0] += 11 * (PAIRS - 1)
            take(PAIRS - 1, link)
            finish_a(PAIRS - 1, link)
            finish_b(PAIRS - 1, link)

        @block.tensor
        def _(pe):
            mm = nc.tensor.matmul
            pe.wait_ge(ident_ready, 1)
            pe.wait_ge(xr_loaded, 32)

            def transpose_xr(k):
                if k >= 2:
                    pe.wait_ge(xrt_saved, k - 1)
                for j in range(GT):
                    last = nc.tensor.transpose(tb[k % 2][:, j * P:(j + 1) * P], xr[:, k * GT + j, :], identf[:, :])
                last.then_inc(xrt_ready, 1)

            transpose_xr(0)
            pe.wait_ge(w_loaded, 16 * 13)
            for k in range(GROUPS):
                if k + 1 < GROUPS:
                    transpose_xr(k + 1)
                pe.wait_ge(xrt_saved, k + 1)
                for j in range(GT):
                    if k and j % 2 == 0:
                        pe.wait_ge(proj_saved, 2 * k - 1 + j // 2)
                    t = k * GT + j
                    lhs = xrt[:, k % 2, j * P:(j + 1) * P]
                    mm(zb[j // 2][:, (j % 2) * WCOLS:(j % 2 + 1) * WCOLS], lhs, w_all[:, :], start=j % 2 == 0, stop=True, skip_group_check=True)
                    last = mm(acc[t // QB][:, (t % QB) * D:(t % QB + 1) * D], lhs, w_agg[:, :], start=t % QB == 0, stop=True, skip_group_check=True)
                    if j % 2:
                        last.then_inc(proj_ready, 1)
            pe.wait_ge(consts, 1)
            pe.wait_ge(cs_ready, 1)
            pe.wait_ge(proj_saved, 2 * GROUPS)
            for k in range(4):
                for i in range(2):
                    if k >= 2:
                        pe.wait_ge([zc_saved, zr_saved][i], k - 1)
                    for j in range(QB):
                        last = nc.tensor.transpose([tb, zb][k % 2][i][:, :].bitcast(bf16)[0:6, j * P:(j + 1) * P],
                                                   cs_parts[:, k * QB + j, 6 * i:6 * i + 6], ident[:, 0, :])
                    last.then_inc(zt_ready, 1)
            pe.wait_ge(zc_saved, 4)
            pe.wait_ge(zr_saved, 4)

            with pe.Fori(0, GROUPS) as g:
                pe.wait_ge(y_split, g + 1)
                for q in range(UNITS):
                    pe.wait_ge(a_loaded[q], g * 16 + 16)
                    for b in range(QB):
                        t, h = b // 2, b % 2
                        pe.wait_ge(z_free, g * (UNITS * QB) + (q * QB + b + 1))
                        mm(zb[h][:, :], z_rows[:, bass.ds(g * GW + t * P, P)], z_cols[:, q * QC + h * ZC:q * QC + (h + 1) * ZC],
                           start=True, stop=True).then_inc(z_ready, 1)
                        s = b // 4
                        if b % 4 == 0:
                            pe.wait_ge(t_free, g * (2 * UNITS) + (2 * q + s + 1))
                        for t in range(GT):
                            lhs = block_t(q, t, b)
                            last = mm(tb[s][:, (b % 4) * P:(b % 4 + 1) * P], lhs, ident[:, t, :],
                                      start=b % 4 == 0 and t == 0, stop=True, skip_group_check=True)
                            if b % 4 == 3 and t == GT - 1:
                                last.then_inc(t_ready, 1)
                            for k in range(3):
                                last = mm(acc[q][:, b * D:(b + 1) * D], lhs,
                                          parts[:, bass.ds(g * GT + t, 1), k * D:(k + 1) * D].rearrange("p g d -> p (g d)"),
                                          start=False, stop=True, skip_group_check=True)
                    last.then_inc(unit_read, 1)

            def transpose_x1(n):
                pe.wait_ge(x1_ready, n + 1)
                if n:
                    pe.wait_ge(x1t_saved, n)
                for j in range(BT):
                    last = nc.tensor.transpose(tb[0][0:D, j * P:(j + 1) * P], x1[:, TILES - (n + 1) * BT + j, :], identf[:, :])
                last.then_inc(x1t_ready, 1)

            def support(n):
                pe.wait_ge(x1t_saved, n + 1)
                if n:
                    pe.wait_ge(s_saved, 2 * n - 1)
                for j in range(BT):
                    last = mm(tb[1][:, j * D:(j + 1) * D], x1t[:, n % 2, j * P:(j + 1) * P], w_l1[:, :], start=j == 0, stop=True, skip_group_check=True)
                last.then_inc(s_ready, 1)

            def unpacked(b, a):
                return stage_bf[:, UNITS - 1 - b // QB, a, b % QB, :]

            def count_up_to(b, a):
                mm(zb[a][:, :], upto[:, :], unpacked(b, a), start=b == TILES - 1, stop=True, skip_group_check=True).then_inc(v_ready, 1)

            def count_beyond(b, a):
                mm(zb[a][:, :], beyond[:, :], unpacked(b, a), start=False, stop=True, skip_group_check=True)

            def count(p, b):
                if b % QB == QB - 1:
                    pe.wait_ge(staged, p * 4 + (4 - b // QB))
                for a in range(2):
                    n = 2 * (TILES - 1 - b) + a
                    if not (isinstance(p, int) and p == 0 and n < 2):
                        pe.wait_ge(w_ready, p * (2 * TILES) + (n - 1))
                    if b < TILES - 1:
                        count_beyond(b + 1, a)
                    count_up_to(b, a)

            def products(p, b):
                for a in range(2):
                    n = 2 * (TILES - 1 - b) + a
                    pe.wait_ge(w_ready, p * (2 * TILES) + (n + 1))
                    if b == TILES - 1:
                        pe.wait_ge(acc_free, p * 4 + (2 * a + 2))
                    for t in range(GT):
                        last = mm(acc[2 * a + t // 2][:, (t % 2) * 3 * D:(t % 2 + 1) * 3 * D],
                                  weights_bf[:, a, b % RING, t * P:(t + 1) * P], parts[:, b, :],
                                  start=b == TILES - 1 and t % 2 == 0, stop=True, skip_group_check=True)
                    last.then_inc(w_used, 1)

            def pair(p, first, last):
                for b in reversed(range(TILES)):
                    if first and b % BT == BT - 1:
                        pe.wait_ge(s_split, BATCHES - b // BT)
                    if first and b == TILES - 1:
                        pe.wait_ge(acc_free, 4)
                    if b >= LEAD:
                        count(p, b - LEAD)
                    elif not last:
                        count(p + 1, b - LEAD + TILES)
                    products(p, b)
                    if first and b >= BT:
                        n = BATCHES - b // BT
                        if b % BT == 3:
                            transpose_x1(n)
                        if b % BT == 2:
                            support(n)

            pe.wait_ge(unit_read, GROUPS * UNITS)
            pe.wait_ge(z_free, GROUPS * UNITS * QB + 2)
            for b in reversed(range(TILES - LEAD, TILES)):
                count(0, b)
            pe.wait_ge(t_free, GROUPS * UNITS * 2 + 2)
            transpose_x1(0)
            support(0)
            pair(0, True, False)
            with pe.Fori(1, PAIRS - 1) as p:
                pair(p, False, False)
            pair(PAIRS - 1, False, True)


_ORDER = ["x", "adj", "L0_gnn_relationship_features", "L0_gnn_W_obj", "L0_gnn_b_obj", "L0_gnn_W_nobj", "L0_gnn_b_nobj",
          "L0_gnn_W_rel", "L0_gnn_b_rel", "L0_gnn_W_skip", "L0_gnn_b_skip", "L0_gnn_Wa_w", "L0_gnn_Wa_b",
          "L1_gnn_weight", "L1_gnn_bias"]


def kernel(**inputs):
    import numpy as np
    import concourse.bacc as bacc
    from concourse.bass_utils import run_bass_kernel_spmd

    nc = bacc.Bacc("TRN2", target_bir_lowering=False, num_devices=1)
    arrays, args = {}, []
    for name in _ORDER:
        a = np.ascontiguousarray(inputs[name])
        arrays[f"in_{name}"] = a
        args.append(nc.dram_tensor(f"in_{name}", a.shape, mybir.dt.from_np(a.dtype), kind="ExternalInput").ap())
    out = nc.dram_tensor("out", (N, D), mybir.dt.float32, kind="ExternalOutput").ap()
    build(nc, *args, out)
    r = run_bass_kernel_spmd(nc, [arrays], core_ids=[0])
    return r.results[0]["out"]
```

```python
from contextlib import ExitStack

import concourse.bass as bass
from concourse import mybir
from concourse.alu_op_type import AluOpType as ALU

N, D, P = 4096, 64, 128
TILES = N // P
GT = 4
GROUPS = TILES // GT
QB = 8
UNITS = TILES // QB
QC = QB * P
ZC = 512
GW = GT * P
PAIRS = GROUPS // 2
PT = 2 * GT
RING = 8
LEAD = RING - 1
BT = 4
BATCHES = TILES // BT
NORMS = 2 + (BATCHES - 2) // 2
XR_PIECES = [slice(TILES - GT, TILES), slice(TILES - QB, TILES - GT)] + [
    slice(u * QB, (u + 1) * QB) for u in reversed(range(UNITS - 1))]
SHARED = slice(0, TILES - PT), slice(TILES - PT, TILES)
MAX_NEIGH = 100
EPS = 1e-5
STEP = 128.0
OWN = 16384.0
SHIFT = 2.0 ** (127 - MAX_NEIGH)
ON = 2.0
WCOLS = 2 * D + 2


def build(nc, x, adj, rel, W_obj, b_obj, W_nobj, b_nobj, W_rel, b_rel, W_skip, b_skip, Wa_w, Wa_b,
          W_l1, b_l1, out):
    fp32, bf16, u16 = mybir.dt.float32, mybir.dt.bfloat16, mybir.dt.uint16
    ACT = mybir.ActivationFunctionType
    AX = mybir.AxisListType.X
    es = ExitStack()
    with es:
        def sb(name, shape, dt):
            return es.enter_context(nc.sbuf_tensor(name, shape, dt))

        def sem(name):
            return es.enter_context(nc.semaphore(name))

        packed = sb("packed", [P, GROUPS, TILES, P], u16)
        area_a = sb("area_a", [P, UNITS, GT, QC], fp32)
        stage = area_a[:, :, :, :].rearrange("p u t c -> p (u t c)").bitcast(u16).rearrange(
            "p (u a b t c) -> p u a b t c", u=UNITS, a=2, b=QB, t=GT)
        stage_bf = area_a[:, :, :, :].rearrange("p u t c -> p (u t c)").bitcast(bf16).rearrange(
            "p (u a b i) -> p u a b i", u=UNITS, a=2, b=QB)
        area_p = sb("area_p", [P, GT * QC], fp32)
        scores = area_p[:, :].rearrange("p (t c) -> p t c", t=GT)
        xr = area_p[:, :].rearrange("p (t c) -> p t c", t=TILES)
        x1 = area_p[:, 0:TILES * D].rearrange("p (t d) -> p t d", t=TILES)
        x1t = area_p[0:D, TILES * D:TILES * D + 2 * GW].rearrange("p (h i) -> p h i", h=2)
        area_y = sb("area_y", [P, TILES, D], fp32)
        base = sb("base", [P, TILES, D], fp32)
        x1b = base
        parts = sb("parts", [P, TILES, 3 * D], bf16)
        y_parts = parts[:, 0:2 * GT, :].rearrange("p (h t) d -> p h t d", h=2)
        z_now = parts[:, 2 * GT:2 * GT + 6, :].rearrange("p t d -> p (t d)")[:, 0:2 * GW].rearrange(
            "p (h i) -> p h i", h=2)
        area_z = sb("area_z", [P, 2, N], bf16)
        z_cols, z_rows = area_z[:, 0, :], area_z[:, 1, :]
        weights_bf = area_z[:, :, :].rearrange("p a (s i) -> p a s i", s=RING)
        weights = weights_bf.bitcast(u16)
        xrt = sb("xrt", [P, 2, GW], fp32)
        tmp_a = xrt[:, 0, :].rearrange("p (t d) -> p t d", t=QB)
        tmp_b = xrt[:, 1, :].rearrange("p (t d) -> p t d", t=QB)
        supp = sb("supp", [P, 2, BT, D], fp32)
        rest = sb("rest", [P, BT, D], fp32)
        rest_y = sb("rest_y", [P, GT, D], fp32)
        identf = sb("identf", [P, P], fp32)
        ident = sb("ident", [P, GT, P], bf16)
        upto = sb("upto", [P, P], bf16)
        beyond = sb("beyond", [P, P], bf16)
        w_all = sb("w_all", [P, WCOLS], fp32)
        w_agg = sb("w_agg", [P, D], fp32)
        w_l1 = sb("w_l1", [D, D], fp32)
        bias = sb("bias", [P, 6, D], fp32)
        wab = sb("wab", [P, 1], fp32)
        floor = sb("floor", [P, 1], fp32)
        cs = sb("cs", [P, 2, TILES], fp32)
        cs_rest = sb("cs_rest", [P, 2, TILES], fp32)
        cs_parts = sb("cs_parts", [P, TILES, 18], bf16)
        top = sb("top", [P, GT, 2], fp32)
        negmax = sb("negmax", [P, TILES, UNITS], fp32)
        sums = sb("sums", [P, TILES, UNITS], fp32)
        small = sb("small", [P, 8, TILES], fp32)
        share = sb("share", [P, TILES, UNITS], fp32)
        ln = sb("ln", [P, 8, QB], fp32)
        root_warm = sb("root_warm", [P, 1], fp32)

        acc = [es.enter_context(nc.psum_tensor(f"acc{i}", [P, 512], fp32)) for i in range(4)]
        zb = [es.enter_context(nc.psum_tensor(f"zb{i}", [P, 512], fp32)) for i in range(2)]
        tb = [es.enter_context(nc.psum_tensor(f"tb{i}", [P, 512], fp32)) for i in range(2)]

        late_loaded, w_agg_loaded = sem("late_loaded"), sem("w_agg_loaded")
        acc_copied = sem("acc_copied")
        b_loaded, agg_ready = sem("b_loaded"), sem("agg_ready")
        w_loaded, zeroed, zeroed_z = sem("w_loaded"), sem("zeroed"), sem("zeroed_z")
        xr_loaded = [sem(f"xr_loaded{k}") for k in range(len(XR_PIECES))]
        ident_ready, consts = sem("ident_ready"), sem("consts")
        a_loaded = [sem(f"a_loaded{q}") for q in range(UNITS)]
        xrt_ready, xrt_saved, proj_ready, proj_saved = sem("xrt_ready"), sem("xrt_saved"), sem("proj_ready"), sem("proj_saved")
        cs_ready, zct_ready, zrt_ready = sem("cs_ready"), sem("zct_ready"), sem("zrt_ready")
        zc_saved, zr_saved = sem("zc_saved"), sem("zr_saved")
        y_saved, y_split = sem("y_saved"), sem("y_split")
        z_ready, z_free = sem("z_ready"), sem("z_free")
        t_ready, t_free = sem("t_ready"), sem("t_free")
        unit_read = sem("unit_read")
        max_ready, p_free = sem("max_ready"), sem("p_free")
        share_in, share_out = sem("share_in"), sem("share_out")
        var_ready, std_ready = sem("var_ready"), sem("std_ready")
        x1_ready, x1t_ready, x1t_saved = sem("x1_ready"), sem("x1t_ready"), sem("x1t_saved")
        s_ready, s_saved, s_split = sem("s_ready"), sem("s_saved"), sem("s_split")
        x1b_ready = sem("x1b_ready")
        staged = sem("staged")
        v_ready, w_ready, w_used = sem("v_ready"), sem("w_ready"), sem("w_used")
        acc_free = sem("acc_free")
        out_ready, out_done = sem("out_ready"), sem("out_done")
        dve_done, pool_done = sem("dve_done"), sem("pool_done")
        passed, passed_pool = sem("passed"), sem("passed_pool")

        adj_v = adj.rearrange("(g t p) c -> p g t c", t=GT, p=P)
        x_v = x.rearrange("(t p) d -> p t d", p=P)
        r_v = rel.rearrange("(t p) d -> p t d", p=P)
        out_v = out.rearrange("(t p) d -> p t d", p=P)

        def block_t(q, t, b):
            v = area_a[:, q, t, b * P:(b + 1) * P].bitcast(bf16)
            return v.rearrange("p (c h) -> p c h", h=2)[:, :, 1]

        def z_chunk(c):
            return slice(N - (c + 1) * QC, N - c * QC)

        def z_bank(c, i):
            return [[acc[0], acc[1]], [acc[0], acc[0]], [tb[0], tb[1]], [zb[0], zb[1]]][c][i]

        def batch_rows(n):
            return slice(TILES - (n + 1) * BT, TILES - n * BT)

        def half_rows(a):
            return slice((1 - a) * GT, (2 - a) * GT)

        def norm_rows(m):
            return batch_rows(m) if m < 2 else slice(TILES - (2 * m) * BT, TILES - (2 * m - 2) * BT)

        def norm_of(n):
            return n if n < 2 else 1 + n // 2

        def support_after(n):
            rows_end = TILES - n * BT
            return {1: rows_end + 2, BATCHES - 1: LEAD}.get(n, rows_end + (2 if n == 2 else 3))

        block = es.enter_context(nc.Block())

        @block.sync
        def _(sp):
            for k, rows in enumerate(XR_PIECES):
                if k == 3:
                    sp.wait_ge(w_loaded, 16 * 4)
                sp.dma_start(xr[:, rows, 0:D], x_v[:, rows, :]).then_inc(xr_loaded[k], 16)
                sp.dma_start(xr[:, rows, D:2 * D], r_v[:, rows, :]).then_inc(xr_loaded[k], 16)
            for q in range(UNITS):
                sp.dma_start(area_a[:, q, :, :], adj_v[:, GROUPS - 1, :, q * QC:(q + 1) * QC]).then_inc(a_loaded[q], 16)
            with sp.Fori(1, GROUPS) as g:
                for q in range(UNITS):
                    sp.wait_ge(unit_read, g * UNITS + (q + 1 - UNITS))
                    sp.wait_ge(z_free, (g * UNITS + (q + 1 - UNITS)) * QB + 2)
                    sp.dma_start(area_a[:, q, :, :], adj_v[:, bass.ds(g * -1 + (GROUPS - 1), 1), :, q * QC:(q + 1) * QC].rearrange("p g t c -> p (g t) c")).then_inc(a_loaded[q], 16)
            with sp.Fori(0, PAIRS - 1) as g:
                sp.wait_ge(out_ready, g + 2)
                rows = bass.ds(g * -PT + (TILES - PT), PT)
                sp.dma_start(out_v[:, rows, :], x1b[:, rows, :]).then_inc(out_done, 16)
            for a in range(2):
                sp.wait_ge(out_ready, PAIRS + 1 + a)
                rows = half_rows(a)
                sp.dma_start(out_v[:, rows, :], x1b[:, rows, :]).then_inc(out_done, 16)
            sp.wait_ge(out_done, 16 * (PAIRS + 1))

        @block.gpsimd
        def _(pool):
            count = [0]

            def link(ins):
                count[0] += 1
                ins.then_inc(pool_done, 1)
                pool.wait_ge(pool_done, count[0])

            def diagonal(tile, fill):
                return nc.gpsimd.affine_select(out=tile, in_=tile, compare_op=ALU.not_equal, fill=fill, base=0,
                                               pattern=[[-1, P]], channel_multiplier=1)

            link(nc.gpsimd.memset(identf[:], 0.0))
            diagonal(identf[:, :], 1.0).then_inc(ident_ready, 1)
            pool.dma_start(w_agg[0:D, :], W_obj).then_inc(w_agg_loaded, 16)
            pool.dma_start(w_agg[D:P, :], W_rel).then_inc(w_agg_loaded, 16)
            pool.dma_start(bias[:, 1, :], b_skip.partition_broadcast(P)).then_inc(b_loaded, 16)
            pool.dma_start(wab[:, :], Wa_b.partition_broadcast(P)).then_inc(b_loaded, 16)
            pool.dma_start(bias[:, 0, :], b_nobj.partition_broadcast(P)).then_inc(b_loaded, 16)
            for k, b in enumerate((b_obj, b_rel, b_l1)):
                pool.dma_start(bias[:, 2 + k, :], b.partition_broadcast(P)).then_inc(late_loaded, 16)
            pool.dma_start(w_l1[:, :], W_l1).then_inc(late_loaded, 16)
            for t in range(GT):
                nc.gpsimd.memset(ident[:, t, :], 0.0)
            nc.gpsimd.memset(floor[:], STEP * (MAX_NEIGH + 1) - OWN)
            nc.gpsimd.memset(upto[:], -STEP / ON)
            link(nc.gpsimd.memset(beyond[:], -STEP / ON))
            for t in range(GT):
                diagonal(ident[:, t, :], 2.0 ** t)
            nc.gpsimd.affine_select(out=upto[:, :], in_=upto[:, :], compare_op=ALU.is_ge, fill=0.0, base=0,
                                    pattern=[[-1, P]], channel_multiplier=1)
            link(nc.gpsimd.affine_select(out=beyond[:, :], in_=beyond[:, :], compare_op=ALU.is_ge, fill=0.0, base=0,
                                         pattern=[[1, P]], channel_multiplier=-1))
            diagonal(upto[:, :], (OWN - STEP) / ON)
            diagonal(beyond[:, :], -OWN / ON).then_inc(consts, 1)
            nc.gpsimd.memset(area_z[:, :, :].bitcast(fp32), 0.0).then_inc(zeroed_z, 1)
            start = count[0]

            def split_y(g, half, first):
                y = area_y[:, bass.ds(g * -GT + (TILES - GT), GT), :]
                hi, mid, lo = (y_parts[:, half, :, k * D:(k + 1) * D] for k in range(3))
                done = g * 3 + start

                def carry():
                    pool.sem_inc(passed_pool, 1)

                if first:
                    pool.wait_ge(y_saved, g + 1)
                else:
                    pool.wait_ge(unit_read, (g - 1) * UNITS)
                    carry()
                nc.gpsimd.tensor_copy(hi, y).then_inc(pool_done, 1)
                pool.wait_ge(pool_done, done + 1)
                carry()
                nc.gpsimd.tensor_tensor(rest_y[:, :, :], y, hi, ALU.subtract).then_inc(pool_done, 1)
                pool.wait_ge(pool_done, done + 2)
                carry()
                nc.gpsimd.tensor_copy(mid, rest_y[:, :, :]).then_inc(pool_done, 1)
                pool.wait_ge(pool_done, done + 3)
                carry()
                nc.gpsimd.tensor_tensor(lo, rest_y[:, :, :], mid, ALU.subtract).then_inc(y_split, 1)
                pool.wait_ge(y_split, g * 2 + 1)
                carry()
                if first:
                    pool.wait_ge(zr_saved, 1)
                nc.gpsimd.tensor_copy(z_now[:, half, :], z_rows[:, bass.ds(g * -GW + (N - GW), GW)]).then_inc(y_split, 1)

            for half in range(2):
                split_y(half, half, True)
            pool.wait_ge(late_loaded, 16 * 4)
            nc.gpsimd.tensor_tensor(bias[:, 5, :], bias[:, 2, :], bias[:, 3, :], ALU.add)
            pool.wait_ge(zr_saved, 4)
            with pool.Fori(1, PAIRS) as gp:
                for half in range(2):
                    split_y(gp * 2 + half, half, False)
            count[0] = start + 3 * GROUPS
            for n in range(BATCHES):
                rows = batch_rows(n)
                hi, mid, lo = (parts[:, rows, k * D:(k + 1) * D] for k in range(3))
                pool.wait_ge(s_saved, 2 * n + 2)
                if n:
                    pool.wait_ge(s_split, n)
                link(nc.gpsimd.tensor_tensor(rest[:, :, :], supp[:, n % 2, :, :], hi, ALU.subtract))
                link(nc.gpsimd.tensor_copy(mid, rest[:, :, :]))
                nc.gpsimd.tensor_tensor(lo, rest[:, :, :], mid, ALU.subtract).then_inc(s_split, 1)
                if n == 0:
                    pool.wait_ge(acc_copied, 1)
                    nc.gpsimd.tensor_tensor(area_y[:, 0:QB, :], area_y[:, 0:QB, :], bias[:, 5:6, :].broadcast_to([P, QB, D]), ALU.add).then_inc(agg_ready, 1)
                pool.wait_ge(x1_ready, norm_of(n) + 1)
                nc.gpsimd.tensor_tensor(x1b[:, rows, :], x1[:, rows, :], bias[:, 4:5, :].broadcast_to([P, BT, D]), ALU.add).then_inc(x1b_ready, 1)

        @block.scalar
        def _(act):
            act.wait_ge(zeroed, 1)
            act.dma_start(w_all[0:D, 0:D], W_nobj).then_inc(w_loaded, 16)
            act.dma_start(w_all[0:D, D:2 * D], W_skip).then_inc(w_loaded, 16)
            act.dma_start(w_all[0:D, 2 * D:2 * D + 1], Wa_w[0:D, :]).then_inc(w_loaded, 16)
            act.dma_start(w_all[D:P, 2 * D + 1:2 * D + 2], Wa_w[D:2 * D, :]).then_inc(w_loaded, 16)

            def save_z_cols(c):
                act.wait_ge(zct_ready, c + 1)
                nc.scalar.activation(z_cols[0:6, z_chunk(c)], z_bank(c, 0)[:, :].bitcast(bf16)[0:6, :], ACT.Copy).then_inc(zc_saved, 1)

            for k in range(GROUPS):
                act.wait_ge(xrt_ready, k + 1)
                if k >= 2:
                    act.wait_ge(proj_ready, k - 1)
                nc.scalar.activation(xrt[:, k % 2, :], tb[k % 2][:, :], ACT.Copy).then_inc(xrt_saved, 1)
                if k == 3:
                    act.wait_ge(zeroed_z, 1)
                if k >= 3 and k % 2:
                    save_z_cols((k - 3) // 2)
            save_z_cols(3)
            act.wait_ge(zc_saved, 4)
            act.wait_ge(zr_saved, 4)
            act.sem_inc(t_free, 2)
            act.sem_inc(p_free, GT)

            def unit(g, q):
                def exps(t):
                    act.wait_ge(max_ready, g * (UNITS * GT) + (q * GT + t + 1))
                    nc.scalar.activation(scores[:, t, :], scores[:, t, :], ACT.Exp,
                                         bias=negmax[:, bass.ds(g * GT + t, 1), q],
                                         accum_out=sums[:, bass.ds(g * GT + t, 1), q]).then_inc(p_free, 1)

                def save_transpose(s):
                    act.wait_ge(t_ready, g * (2 * UNITS) + (2 * q + s + 1))
                    nc.scalar.activation(
                        packed[:, bass.ds(g, 1), q * QB + s * 4:q * QB + s * 4 + 4, :].rearrange("p g b i -> p (g b i)"),
                        tb[s][:, :], ACT.Copy).then_inc(t_free, 1)

                exps(0)
                save_transpose(0)
                exps(1)
                exps(2)
                save_transpose(1)
                exps(3)

            def share_exp(part):
                act.wait_ge(share_in, part + 1)
                nc.scalar.activation(share[:, SHARED[part], :], share[:, SHARED[part], :], ACT.Exp).then_inc(share_out, 1)

            with act.Fori(0, PAIRS - 1) as gp:
                for half in range(2):
                    for q in range(UNITS):
                        unit(gp * 2 + half, q)
            for g in (GROUPS - 2, GROUPS - 1):
                for q in range(UNITS):
                    unit(g, q)
                    if (g, q) == (GROUPS - 2, 1):
                        share_exp(0)
            share_exp(1)

            def std(m):
                w = norm_rows(m).stop - norm_rows(m).start
                act.wait_ge(var_ready, m + 1)
                nc.scalar.activation(ln[:, 2, 0:w], ln[:, 1, 0:w], ACT.Sqrt).then_inc(std_ready, 1)

            def std_pair(p):
                act.wait_ge(var_ready, p + (NORMS + 1))
                nc.scalar.activation(ln[:, 2, :], ln[:, 1, :], ACT.Sqrt).then_inc(std_ready, 1)

            def save_x1t(n):
                act.wait_ge(x1t_ready, n + 1)
                if n >= 2:
                    act.wait_ge(s_ready, n - 1)
                nc.scalar.activation(x1t[:, n % 2, :], tb[0][0:D, :], ACT.Copy).then_inc(x1t_saved, 1)

            def save_support(n):
                act.wait_ge(s_ready, n + 1)
                if n >= 2:
                    act.wait_ge(s_split, n - 1)
                nc.scalar.activation(supp[:, n % 2, :, :].rearrange("p t d -> p (t d)"), tb[1][:, 0:BT * D], ACT.Copy, scale=SHIFT).then_inc(s_saved, 1)
                act.wait_ge(s_saved, 2 * n + 1)
                nc.scalar.activation(parts[:, TILES - (n + 1) * BT:TILES - n * BT, 0:D], supp[:, n % 2, :, :], ACT.Copy).then_inc(s_saved, 1)

            def weigh(p, b, first):
                for a in range(2):
                    n = 2 * (TILES - 1 - b) + a
                    act.wait_ge(v_ready, p * (2 * TILES) + (n + 1))
                    if not (first and n < 2 * RING):
                        act.wait_ge(w_used, p * (2 * TILES) + (n + 1 - 2 * RING))
                    nc.scalar.activation(weights[:, a, b % RING, :], zb[a][:, :], ACT.Relu, bias=floor[:, 0:1]).then_inc(w_ready, 1)

            for b in reversed(range(TILES - LEAD, TILES)):
                if b == TILES - 3:
                    nc.scalar.activation(root_warm[:, :], floor[:, :], ACT.Sqrt, scale=-1.0)
                    std(0)
                    act.wait_ge(unit_read, GROUPS * UNITS)
                    act.wait_ge(y_split, 2 * GROUPS)
                    nc.scalar.activation(area_y[:, 0:QB, :].rearrange("p t d -> p (t d)"), acc[0][:, :], ACT.Copy).then_inc(acc_copied, 1)
                if b == TILES - 4:
                    save_x1t(0)
                if b == TILES - 5:
                    save_support(0)
                if b == TILES - LEAD:
                    std(1)
                weigh(0, b, True)
            for b in reversed(range(-1, TILES - LEAD)):
                for n in range(1, BATCHES):
                    if b + LEAD == support_after(n):
                        save_x1t(n)
                    if b + LEAD == support_after(n) - 1:
                        save_support(n)
                    if n > 1 and n % 2 == 0 and b + LEAD == TILES - (n - 1) * BT:
                        std(norm_of(n))
                if b >= 0:
                    weigh(0, b, True)
            with act.Fori(1, PAIRS) as p:
                for b in reversed(range(TILES)):
                    weigh(p, b, False)
                    if b == TILES - 4 - LEAD:
                        std_pair(p - 1)
            for a in range(2):
                act.wait_ge(var_ready, NORMS + PAIRS + a)
                nc.scalar.activation(ln[:, 2, half_rows(a)], ln[:, 1, half_rows(a)], ACT.Sqrt).then_inc(std_ready, 1)

        @block.vector
        def _(dve):
            count = [0]

            def link(ins):
                count[0] += 1
                ins.then_inc(dve_done, 1)
                dve.wait_ge(dve_done, count[0])

            nc.vector.memset(w_all[:], 0.0).then_inc(zeroed, 1)
            nc.vector.memset(cs_parts[:, :, 3:9], 1.0)
            dve.wait_ge(b_loaded, 16 * 3)
            def split_cs(c):
                rows = slice(TILES - (c + 1) * QB, TILES - c * QB)
                hi, mid, lo = (cs_parts[:, rows, :].rearrange("p t (k c) -> p k t c", k=2)[:, :, :, k] for k in range(3))
                dve.wait_ge(proj_saved, 4 * c + 4)
                link(nc.vector.tensor_copy(hi, cs[:, :, rows]))
                link(nc.vector.tensor_tensor(cs_rest[:, :, rows], cs[:, :, rows], hi, ALU.subtract))
                link(nc.vector.tensor_copy(mid, cs_rest[:, :, rows]))
                nc.vector.tensor_tensor(lo, cs_rest[:, :, rows], mid, ALU.subtract).then_inc(cs_ready, 1)

            def save_z_rows(c):
                dve.wait_ge(zrt_ready, c + 1)
                nc.vector.tensor_copy(z_rows[0:6, z_chunk(c)], z_bank(c, 1)[:, :].bitcast(bf16)[0:6, :]).then_inc(zr_saved, 1)

            for k in range(GROUPS):
                if k % 2 == 0:
                    rows = slice(TILES - (k + 2) * GT, TILES - k * GT)
                    for n, piece in enumerate(XR_PIECES):
                        if rows.start <= piece.start < rows.stop:
                            dve.wait_ge(xr_loaded[n], 32)
                    link(nc.vector.tensor_tensor(base[:, rows, :], xr[:, rows, 0:D], bias[:, 1:2, :].broadcast_to([P, 2 * GT, D]), ALU.add))
                for h in range(2):
                    dve.wait_ge(proj_ready, 2 * k + h + 1)
                    rows = slice(TILES - (k + 1) * GT + 2 * h, TILES - (k + 1) * GT + 2 * h + 2)
                    z = zb[h][:, 0:2 * WCOLS].rearrange("p (t c) -> p t c", t=2)
                    nc.vector.tensor_copy(cs[:, 0, rows], z[:, :, 2 * D + 1])
                    nc.vector.tensor_scalar(cs[:, 1, rows], z[:, :, 2 * D], wab[:, 0:1], None, ALU.add)
                    y = nc.vector.tensor_tensor(area_y[:, rows, :], z[:, :, 0:D], bias[:, 0:1, :].broadcast_to([P, 2, D]), ALU.add)
                    if h:
                        y.then_inc(y_saved, 1)
                    nc.vector.tensor_tensor(base[:, rows, :], z[:, :, D:2 * D], base[:, rows, :], ALU.add).then_inc(proj_saved, 1)
                    if (k, h) == (2, 1):
                        dve.wait_ge(zeroed_z, 1)
                        save_z_rows(0)
                    if (k, h) == (5, 0):
                        save_z_rows(1)
                if k % 2:
                    split_cs(k // 2)
            save_z_rows(2)
            save_z_rows(3)
            dve.wait_ge(zc_saved, 4)
            dve.wait_ge(zr_saved, 4)
            dve.sem_inc(z_free, 2)

            def unit(g, q, prompt=False, extra=iter(())):
                dve.wait_ge(a_loaded[q], g * 16 + 16)
                first = g * (UNITS * QB) + q * QB

                def neg_max(t):
                    dve.wait_ge(z_free, first + (2 * t + 4))
                    nc.vector.tensor_scalar(negmax[:, bass.ds(g * GT + t, 1), q], top[:, t, 0:1], top[:, t, 1:2], -1.0,
                                            ALU.max, ALU.mult).then_inc(max_ready, 1)

                for t in range(GT):
                    dve.wait_ge(p_free, g * (UNITS * GT) + (q * GT + t + 1))
                    for h in range(2):
                        dve.wait_ge(z_ready, first + (2 * t + h + 1))
                        cols = slice(h * ZC, (h + 1) * ZC)
                        dve.sem_inc(passed, 1)
                        nc.vector.tensor_tensor_reduce(out=scores[:, t, cols], in0=area_a[:, q, t, cols], in1=zb[h][:, :],
                                                       scale=1.0, scalar=-3.0e38, op0=ALU.mult, op1=ALU.max,
                                                       accum_out=top[:, t, h:h + 1]).then_inc(z_free, 1)
                    if prompt:
                        neg_max(t)
                    elif t:
                        neg_max(t - 1)
                    next(extra, None)
                if not prompt:
                    neg_max(GT - 1)

            def unpack_ops(p, c, done):
                for a in range(2):
                    src = packed[:, bass.ds(p * 2 + a, 1), c * QB:(c + 1) * QB, :].rearrange("p g b i -> p (g b) i")
                    for t in range(GT):
                        ins = nc.vector.tensor_scalar(stage[:, UNITS - 1 - c, a, :, t, :], src, 1 << t, 14 - t,
                                                      ALU.bitwise_and, ALU.logical_shift_left)
                        if (a, t) == (1, GT - 1):
                            ins.then_inc(done, 1)
                        yield

            def unpack(p, c, first):
                if not first:
                    dve.wait_ge(v_ready, p * (2 * TILES) + (2 * (1 - c * QB) if c else 0))
                for _ in unpack_ops(p, c, staged):
                    pass

            def paced(ops):
                for ins in ops:
                    count[0] += 1
                    mine = count[0]
                    ins.then_inc(dve_done, 1)
                    yield
                    dve.wait_ge(dve_done, mine)

            def share_a(part):
                w = SHARED[part]
                n = w.stop - w.start
                low = small[:, 0, w]
                dve.wait_ge(max_ready, w.stop * UNITS)
                yield nc.vector.tensor_reduce(low, negmax[:, w, :], AX, ALU.min)
                nc.vector.tensor_tensor(share[:, w, :], low.unsqueeze(2).broadcast_to([P, n, UNITS]), negmax[:, w, :],
                                        ALU.subtract).then_inc(share_in, 1)

            def share_b(part):
                w = SHARED[part]
                n = w.stop - w.start
                total, inverse = small[:, 1, w], small[:, 2, w]
                dve.wait_ge(share_out, part + 1)
                dve.wait_ge(p_free, w.stop * UNITS + GT)
                yield nc.vector.tensor_tensor(share[:, w, :], share[:, w, :], sums[:, w, :], ALU.mult)
                yield nc.vector.tensor_reduce(total, share[:, w, :], AX, ALU.add)
                yield nc.vector.reciprocal(inverse, total)
                yield nc.vector.tensor_tensor(share[:, w, :], share[:, w, :], inverse.unsqueeze(2).broadcast_to([P, n, UNITS]), ALU.mult)
                yield nc.vector.tensor_reduce(small[:, 3, w], share[:, w, :], AX, ALU.add)

            def rho(t):
                t = (GROUPS - 1 - t // GT) * GT + t % GT
                return small[:, 3, t:t + 1]

            with dve.Fori(0, PAIRS - 1) as gp:
                for half in range(2):
                    for q in range(UNITS):
                        unit(gp * 2 + half, q)
            g = GROUPS - 2
            unit(g, 0, extra=paced(share_a(0)))
            unit(g, 1)
            work = paced(share_b(0))
            unit(g, 2, extra=work)
            unit(g, 3, extra=work)
            unit(g + 1, 0)
            dve.wait_ge(unit_read, GROUPS * UNITS - UNITS + 1)
            dve.wait_ge(z_free, (GROUPS * UNITS - UNITS + 1) * QB + 2)
            dve.wait_ge(t_free, 2 * UNITS * 2 + 2)
            work = unpack_ops(0, UNITS - 1, staged)
            unit(g + 1, 1, extra=work)
            unit(g + 1, 2, extra=work)
            unit(g + 1, 3, prompt=True)
            assert next(work, None) is None
            dve.wait_ge(z_free, GROUPS * UNITS * QB + 2)
            for ins in share_a(1):
                link(ins)
            dve.wait_ge(unit_read, GROUPS * UNITS)
            dve.wait_ge(y_split, 2 * GROUPS)

            def save_aggregate(m):
                nc.vector.tensor_tensor(area_y[:, m * QB:(m + 1) * QB, :], acc[m][:, :].rearrange("p (t d) -> p t d", t=QB),
                                        bias[:, 5:6, :].broadcast_to([P, QB, D]), ALU.add).then_inc(acc_free, 1)

            save_aggregate(3)

            def norm_a(y, at):
                total, var, square = ln[:, 0, at], ln[:, 1, at], tmp_b[:, at, :]
                spread = [P, at.stop - at.start, D]
                yield nc.vector.tensor_reduce(total, y, AX, ALU.add)
                yield nc.vector.scalar_tensor_tensor(y, total.unsqueeze(2).broadcast_to(spread), -1.0 / D, y, ALU.mult, ALU.add)
                yield nc.vector.tensor_tensor(square, y, y, ALU.mult)
                yield nc.vector.tensor_reduce(var, square, AX, ALU.add)
                nc.vector.tensor_scalar(var, var, 1.0 / D, EPS, ALU.mult, ALU.add).then_inc(var_ready, 1)

            def norm_b(y, dst, at, done):
                var, root, inv, half = (ln[:, k, at] for k in range(1, 5))
                yield nc.vector.reciprocal(inv, root)
                yield nc.vector.tensor_tensor(half, var, inv, ALU.mult)
                yield nc.vector.scalar_tensor_tensor(half, half, -0.5, inv, ALU.mult, ALU.mult)
                yield nc.vector.scalar_tensor_tensor(inv, half, 1.5, inv, ALU.add, ALU.mult)
                nc.vector.tensor_tensor(dst, y, inv.unsqueeze(2).broadcast_to([P, at.stop - at.start, D]), ALU.mult).then_inc(done, 1)

            def batch_a(m):
                rows = norm_rows(m)
                w = rows.stop - rows.start
                dve.wait_ge(acc_free, min(m, 2) + 1)
                if m:
                    dve.wait_ge(x1_ready, m)
                if m == NORMS - 1:
                    dve.wait_ge(agg_ready, 1)
                for j in range(w):
                    t = rows.start + j
                    last = nc.vector.scalar_tensor_tensor(tmp_a[:, j, :], area_y[:, t, :], rho(t), base[:, t, :], ALU.mult, ALU.add)
                link(last)
                for ins in norm_a(tmp_a[:, 0:w, :], slice(0, w)):
                    link(ins)

            def batch_b(m):
                rows = norm_rows(m)
                w = rows.stop - rows.start
                dve.wait_ge(std_ready, m + 1)
                for ins in norm_b(tmp_a[:, 0:w, :], x1[:, rows, :], slice(0, w), x1_ready):
                    link(ins)

            batch_a(0)
            save_aggregate(2)
            batch_b(0)
            save_aggregate(1)
            for ins in share_b(1):
                link(ins)
            unpack(0, 2, True)
            for m in range(1, NORMS):
                batch_a(m)
                batch_b(m)
                if m == 2:
                    dve.wait_ge(acc_copied, 1)
                    dve.sem_inc(acc_free, 1)
                    unpack(0, 1, True)
                if m == 3:
                    unpack(0, 0, True)

            def take(a, used):
                dve.wait_ge(w_used, used)
                for h in range(2):
                    at = (1 - a) * GT + 2 * h
                    nc.vector.tensor_reduce(tmp_a[:, at:at + 2, :],
                                            acc[2 * a + h][:, 0:6 * D].rearrange("p (t k d) -> p t d k", t=2, k=3),
                                            AX, ALU.add).then_inc(acc_free, 1)

            def finish_a(rows, at):
                yield nc.vector.tensor_tensor(tmp_a[:, at, :], tmp_a[:, at, :], x1b[:, rows, :], ALU.add)
                yield from norm_a(tmp_a[:, at, :], at)

            def finish_b(rows, at):
                yield from norm_b(tmp_a[:, at, :], x1b[:, rows, :], at, out_ready)

            dve.wait_ge(x1_ready, NORMS)
            dve.sem_inc(out_ready, 1)
            before, STEPS = count[0], 9
            with dve.Fori(1, PAIRS) as p:
                here = [0]

                def step(ins):
                    here[0] += 1
                    ins.then_inc(dve_done, 1)
                    dve.wait_ge(dve_done, p * STEPS + (before - STEPS + here[0]))

                for c in (3, 2, 1):
                    unpack(p, c, False)
                rows, whole = bass.ds(p * -PT + TILES, PT), slice(0, PT)
                dve.wait_ge(out_ready, p)
                for a in range(2):
                    take(a, p * (2 * TILES) + (a - 1))
                dve.wait_ge(acc_free, p * 4 + 4)
                dve.wait_ge(x1b_ready, BATCHES)
                for ins in finish_a(rows, whole):
                    step(ins)
                unpack(p, 0, False)
                dve.wait_ge(std_ready, p + NORMS)
                for ins in finish_b(rows, whole):
                    step(ins)
                assert here[0] == STEPS
            count[0] += STEPS * (PAIRS - 1)
            dve.wait_ge(out_ready, PAIRS)

            def last_group(a):
                rows = half_rows(a)
                take(a, PAIRS * 2 * TILES - (1 - a) * LEAD)
                dve.wait_ge(acc_free, PAIRS * 4 + 2 + 2 * a)
                yield from finish_a(rows, rows)
                dve.wait_ge(std_ready, NORMS + PAIRS + a)
                yield from finish_b(rows, rows)

            groups = [paced(last_group(0)), paced(last_group(1))]
            for a in [0] * 3 + [1, 0] * (STEPS - 2) + [1] * 3:
                next(groups[a], None)

        @block.tensor
        def _(pe):
            mm = nc.tensor.matmul
            pe.wait_ge(ident_ready, 1)

            def transpose_xr(k):
                if k >= 2:
                    pe.wait_ge(xrt_saved, k - 1)
                for n, piece in enumerate(XR_PIECES):
                    if piece.stop == TILES - k * GT:
                        pe.wait_ge(xr_loaded[n], 32)
                for j in range(GT):
                    last = nc.tensor.transpose(tb[k % 2][:, j * P:(j + 1) * P], xr[:, TILES - (k + 1) * GT + j, :], identf[:, :])
                last.then_inc(xrt_ready, 1)

            def transpose_z(c, i):
                pe.wait_ge(cs_ready, c + 1)
                for j in range(QB):
                    last = nc.tensor.transpose(z_bank(c, i)[:, :].bitcast(bf16)[0:6, j * P:(j + 1) * P],
                                               cs_parts[:, TILES - (c + 1) * QB + j, 6 * i:6 * i + 6], ident[:, 0, :])
                last.then_inc([zct_ready, zrt_ready][i], 1)

            transpose_xr(0)
            pe.wait_ge(w_loaded, 16 * 4)
            pe.wait_ge(w_agg_loaded, 16 * 2)
            for k in range(GROUPS):
                if k + 1 < GROUPS:
                    transpose_xr(k + 1)
                pe.wait_ge(xrt_saved, k + 1)
                if k == 4:
                    pe.wait_ge(zr_saved, 1)
                if k == 6:
                    pe.wait_ge(zr_saved, 2)
                for j in range(GT):
                    if k and j % 2 == 0:
                        pe.wait_ge(proj_saved, 2 * k - 1 + j // 2)
                    t = TILES - (k + 1) * GT + j
                    lhs = xrt[:, k % 2, j * P:(j + 1) * P]
                    mm(zb[j // 2][:, (j % 2) * WCOLS:(j % 2 + 1) * WCOLS], lhs, w_all[:, :], start=j % 2 == 0, stop=True, skip_group_check=True)
                    last = mm(acc[t // QB][:, (t % QB) * D:(t % QB + 1) * D], lhs, w_agg[:, :], start=k % 2 == 0 and j == 0, stop=True, skip_group_check=True)
                    if j % 2:
                        last.then_inc(proj_ready, 1)
                    if (k, j) == (2, 3):
                        pe.wait_ge(consts, 1)
                        transpose_z(0, 0)
                        transpose_z(0, 1)
                    if (k, j) == (4, 3):
                        pe.wait_ge(zc_saved, 1)
                        transpose_z(1, 0)
                    if (k, j) == (5, 1):
                        pe.wait_ge(zc_saved, 2)
                        transpose_z(1, 1)
                    if (k, j) == (6, 3):
                        transpose_z(2, 0)
            pe.wait_ge(xrt_saved, GROUPS)
            transpose_z(2, 1)
            pe.wait_ge(proj_saved, 2 * GROUPS)
            transpose_z(3, 0)
            transpose_z(3, 1)
            pe.wait_ge(zc_saved, 4)
            pe.wait_ge(zr_saved, 4)

            def unit(g, half, q):
                pe.wait_ge(a_loaded[q], g * 16 + 16)
                for b in range(QB):
                    t, h = b // 2, b % 2
                    pe.wait_ge(z_free, g * (UNITS * QB) + (q * QB + b + 1))
                    mm(zb[h][:, :], z_now[:, half, t * P:(t + 1) * P], z_cols[:, q * QC + h * ZC:q * QC + (h + 1) * ZC],
                       start=True, stop=True).then_inc(z_ready, 1)
                    s = b // 4
                    if b % 4 == 0:
                        pe.wait_ge(t_free, g * (2 * UNITS) + (2 * q + s + 1))
                    for t in range(GT):
                        lhs = block_t(q, t, b)
                        last = mm(tb[s][:, (b % 4) * P:(b % 4 + 1) * P], lhs, ident[:, t, :],
                                  start=b % 4 == 0 and t == 0, stop=True, skip_group_check=True)
                        if b % 4 == 3 and t == GT - 1:
                            last.then_inc(t_ready, 1)
                        for k in range(3):
                            last = mm(acc[q][:, b * D:(b + 1) * D], lhs, y_parts[:, half, t, k * D:(k + 1) * D],
                                      start=False, stop=True, skip_group_check=True)
                last.then_inc(unit_read, 1)

            with pe.Fori(0, PAIRS) as gp:
                for half in range(2):
                    g = gp * 2 + half
                    pe.wait_ge(y_split, g * 2 + 2)
                    for q in range(UNITS):
                        unit(g, half, q)

            def transpose_x1(n):
                pe.wait_ge(x1_ready, norm_of(n) + 1)
                if n:
                    pe.wait_ge(x1t_saved, n)
                for j in range(BT):
                    last = nc.tensor.transpose(tb[0][0:D, j * P:(j + 1) * P], x1[:, TILES - (n + 1) * BT + j, :], identf[:, :])
                last.then_inc(x1t_ready, 1)

            def support(n):
                pe.wait_ge(x1t_saved, n + 1)
                if n:
                    pe.wait_ge(s_saved, 2 * n - 1)
                for j in range(BT):
                    last = mm(tb[1][:, j * D:(j + 1) * D], x1t[:, n % 2, j * P:(j + 1) * P], w_l1[:, :], start=j == 0, stop=True, skip_group_check=True)
                last.then_inc(s_ready, 1)

            def unpacked(b, a):
                return stage_bf[:, UNITS - 1 - b // QB, a, b % QB, :]

            def count_up_to(b, a):
                mm(zb[a][:, :], upto[:, :], unpacked(b, a), start=b == TILES - 1, stop=True, skip_group_check=True).then_inc(v_ready, 1)

            def count_beyond(b, a):
                mm(zb[a][:, :], beyond[:, :], unpacked(b, a), start=False, stop=True, skip_group_check=True)

            def count(p, b):
                if b % QB == QB - 1:
                    pe.wait_ge(staged, p * 4 + (4 - b // QB))
                for a in range(2):
                    n = 2 * (TILES - 1 - b) + a
                    if not (isinstance(p, int) and p == 0 and n < 2):
                        pe.wait_ge(w_ready, p * (2 * TILES) + (n - 1))
                    if b < TILES - 1:
                        count_beyond(b + 1, a)
                    count_up_to(b, a)

            def products(p, b, groups=range(2)):
                for a in groups:
                    n = 2 * (TILES - 1 - b) + a
                    pe.wait_ge(w_ready, p * (2 * TILES) + (n + 1))
                    for t in range(GT):
                        if b == TILES - 1 and t % 2 == 0 and not (isinstance(p, int) and p == 0):
                            pe.wait_ge(acc_free, p * 4 + (2 * a + t // 2 + 1))
                        last = mm(acc[2 * a + t // 2][:, (t % 2) * 3 * D:(t % 2 + 1) * 3 * D],
                                  weights_bf[:, a, b % RING, t * P:(t + 1) * P], parts[:, b, :],
                                  start=b == TILES - 1 and t % 2 == 0, stop=True, skip_group_check=True)
                    last.then_inc(w_used, 1)

            def pair(p, first, last):
                for b in reversed(range(LEAD if last else 0, TILES)):
                    if first and b % BT == BT - 1:
                        pe.wait_ge(s_split, BATCHES - b // BT)
                    if first and b == TILES - 1:
                        pe.wait_ge(acc_free, UNITS - 1)
                        pe.wait_ge(acc_copied, 1)
                    if b >= LEAD:
                        count(p, b - LEAD)
                    else:
                        count(p + 1, b - LEAD + TILES)
                    products(p, b)
                    if first:
                        for n in range(1, BATCHES):
                            if b == support_after(n) + 1:
                                transpose_x1(n)
                            if b == support_after(n):
                                support(n)
                if last:
                    for a in range(2):
                        for b in reversed(range(LEAD)):
                            products(p, b, [a])

            pe.wait_ge(unit_read, GROUPS * UNITS)
            pe.wait_ge(z_free, GROUPS * UNITS * QB + 2)
            for b in reversed(range(TILES - LEAD, TILES)):
                count(0, b)
                if b == TILES - 3:
                    pe.wait_ge(t_free, GROUPS * UNITS * 2 + 2)
                    transpose_x1(0)
                if b == TILES - 4:
                    support(0)
            pair(0, True, False)
            with pe.Fori(1, PAIRS - 1) as p:
                pair(p, False, False)
            pair(PAIRS - 1, False, True)


_ORDER = ["x", "adj", "L0_gnn_relationship_features", "L0_gnn_W_obj", "L0_gnn_b_obj", "L0_gnn_W_nobj", "L0_gnn_b_nobj",
          "L0_gnn_W_rel", "L0_gnn_b_rel", "L0_gnn_W_skip", "L0_gnn_b_skip", "L0_gnn_Wa_w", "L0_gnn_Wa_b",
          "L1_gnn_weight", "L1_gnn_bias"]


def kernel(**inputs):
    import numpy as np
    import concourse.bacc as bacc
    from concourse.bass_utils import run_bass_kernel_spmd

    nc = bacc.Bacc("TRN2", target_bir_lowering=False, num_devices=1)
    arrays, args = {}, []
    for name in _ORDER:
        a = np.ascontiguousarray(inputs[name])
        arrays[f"in_{name}"] = a
        args.append(nc.dram_tensor(f"in_{name}", a.shape, mybir.dt.from_np(a.dtype), kind="ExternalInput").ap())
    out = nc.dram_tensor("out", (N, D), mybir.dt.float32, kind="ExternalOutput").ap()
    build(nc, *args, out)
    r = run_bass_kernel_spmd(nc, [arrays], core_ids=[0])
    return r.results[0]["out"]
```
